# Optimizing a Trainium2 kernel written in Bass

```python
import numpy as np
import jax
import jax.numpy as jnp

def _softmax(x, axis=-1):
    return jax.nn.softmax(x, axis=axis)

def _gelu(x):
    return jax.nn.gelu(x, approximate=True)

def _silu(x):
    return jax.nn.silu(x)

def _sigmoid(x):
    return jax.nn.sigmoid(x)

def _layernorm(x, axis=-1, eps=1e-05):
    m = jnp.mean(x, axis=axis, keepdims=True)
    v = jnp.var(x, axis=axis, keepdims=True)
    return (x - m) / jnp.sqrt(v + eps)

def _scatter_add(tgt, idx, src, axis=0):
    return tgt.at[idx].add(src)

def _segment_sum(src, seg, n):
    return jax.ops.segment_sum(src, seg, n)
kernel_name = 'mk_prb_d1_jaxref_r4_ac90a2'

def setup_inputs(seed: int=0):
    np.random.seed(seed)
    _w = jnp.asarray

    def _L0_attn_setup():
        import jax, jax.numpy as jnp
        import numpy as np
        EMBED_DIM = 256
        NUM_HEADS = 16
        HEAD_DIM = EMBED_DIM // NUM_HEADS
        B, T = (2, 512)
        key = jax.random.key(seed)
        ks = jax.random.split(key, 7)
        s = 0.02
        return {'x': jax.random.normal(ks[0], (B, T, EMBED_DIM), dtype=jnp.float32), 'Wq': jax.random.normal(ks[1], (EMBED_DIM, EMBED_DIM), dtype=jnp.float32) * s, 'bq': jax.random.normal(ks[2], (EMBED_DIM,), dtype=jnp.float32) * s, 'Wkv': jax.random.normal(ks[3], (2 * HEAD_DIM, EMBED_DIM), dtype=jnp.float32) * s, 'bkv': jax.random.normal(ks[4], (2 * HEAD_DIM,), dtype=jnp.float32) * s, 'Wo': jax.random.normal(ks[5], (EMBED_DIM, EMBED_DIM), dtype=jnp.float32) * s, 'bo': jax.random.normal(ks[6], (EMBED_DIM,), dtype=jnp.float32) * s}
    _L0_attn_in = _L0_attn_setup()

    def _L0_ffn_setup():
        import jax, jax.numpy as jnp
        import numpy as np
        from jax import lax
        TOP_K = 1
        key = jax.random.key(seed)
        ks = jax.random.split(key, 9)
        B, N, C = (4, 512, 256)
        E, L, R = (6, 100, 16)
        return {'feats': jax.random.normal(ks[0], (B, N, C), jnp.float32), 'A': jax.random.normal(ks[1], (E, L, R), jnp.float32) * 0.05, 'B': jax.random.normal(ks[2], (E, R, C), jnp.float32) * 0.05, 'w_gate': jax.random.normal(ks[3], (C, E), jnp.float32) * 0.02, 'wt_w': jax.random.normal(ks[4], (C, C), jnp.float32) * (1.0 / np.sqrt(C)), 'wt_b': jax.random.normal(ks[5], (C,), jnp.float32) * 0.01, 'wd_w': jax.random.normal(ks[6], (C, C), jnp.float32) * (1.0 / np.sqrt(C)), 'wd_b': jax.random.normal(ks[7], (C,), jnp.float32) * 0.01, 'scale': jnp.full((1,), 0.001, jnp.float32)}
    _L0_ffn_in = _L0_ffn_setup()
    _d = {'L0_attn_x': _L0_attn_in['x'], 'L0_attn_Wq': _L0_attn_in['Wq'], 'L0_attn_bq': _L0_attn_in['bq'], 'L0_attn_Wkv': _L0_attn_in['Wkv'], 'L0_attn_bkv': _L0_attn_in['bkv'], 'L0_attn_Wo': _L0_attn_in['Wo'], 'L0_attn_bo': _L0_attn_in['bo'], 'L0_ffn_A': _L0_ffn_in['A'], 'L0_ffn_B': _L0_ffn_in['B'], 'L0_ffn_w_gate': _L0_ffn_in['w_gate'], 'L0_ffn_wt_w': _L0_ffn_in['wt_w'], 'L0_ffn_wt_b': _L0_ffn_in['wt_b'], 'L0_ffn_wd_w': _L0_ffn_in['wd_w'], 'L0_ffn_wd_b': _L0_ffn_in['wd_b'], 'L0_ffn_scale': _L0_ffn_in['scale']}
    _x0 = _d['L0_attn_x']
    _d['L0_attn_x'] = jax.random.normal(jax.random.fold_in(jax.random.key(seed), 1), (16, 512, 256), dtype=_x0.dtype)
    del _x0
    return _d

def reference(L0_attn_x, L0_attn_Wq, L0_attn_bq, L0_attn_Wkv, L0_attn_bkv, L0_attn_Wo, L0_attn_bo, L0_ffn_A, L0_ffn_B, L0_ffn_w_gate, L0_ffn_wt_w, L0_ffn_wt_b, L0_ffn_wd_w, L0_ffn_wd_b, L0_ffn_scale):

    def _L0_attn_ref(x, Wq, bq, Wkv, bkv, Wo, bo):
        import jax, jax.numpy as jnp
        import numpy as np
        EMBED_DIM = 256
        NUM_HEADS = 16
        HEAD_DIM = EMBED_DIM // NUM_HEADS
        B, T = (2, 512)
        bsz, tgt_len, _ = x.shape
        scaling = HEAD_DIM ** (-0.5)
        q = (jnp.einsum('bte,oe->bto', x, Wq) + bq) * scaling
        kv = jnp.einsum('bte,oe->bto', x, Wkv) + bkv
        k, v = (kv[..., :HEAD_DIM], kv[..., HEAD_DIM:])
        qr = q.reshape(bsz, NUM_HEADS * tgt_len, HEAD_DIM)
        attn_weights = jnp.einsum('brd,bsd->brs', qr, k)
        attn_probs = jax.nn.softmax(attn_weights, axis=-1)
        attn_output = jnp.einsum('brs,bsd->brd', attn_probs, v)
        attn_output = attn_output.reshape(bsz, NUM_HEADS, tgt_len, HEAD_DIM)
        attn_output = attn_output.transpose(0, 2, 1, 3).reshape(bsz, tgt_len, EMBED_DIM)
        out = jnp.einsum('bte,oe->bto', attn_output, Wo) + bo
        return out

    def _L0_ffn_ref(feats, A, B, w_gate, wt_w, wt_b, wd_w, wd_b, scale):
        import jax, jax.numpy as jnp
        import numpy as np
        from jax import lax
        TOP_K = 1
        Bsz, N, C = feats.shape
        x = feats.reshape(-1, C)
        n = x.shape[0]
        logits = x @ w_gate
        top_vals, top_idx = lax.top_k(logits, TOP_K)
        top_g = jax.nn.softmax(top_vals, axis=-1)
        gates = jnp.zeros_like(logits).at[jnp.arange(n)[:, None], top_idx].set(top_g)
        tokens = jnp.einsum('elr,erc->elc', A, B)
        attn = jnp.einsum('nc,elc->nel', x, tokens) * C ** (-0.5)
        attn = jax.nn.softmax(attn, axis=-1)
        val = jnp.einsum('elc,dc->eld', tokens, wt_w) + wt_b
        delta_f = jnp.einsum('nel,eld->ned', attn[:, :, 1:], val[:, 1:, :])
        delta = (jnp.einsum('ned,cd->nec', delta_f + x[:, None, :], wd_w) + wd_b) * scale[0]
        combined = jnp.sum(jnp.exp(delta) * gates[:, :, None], axis=1)
        combined = jnp.where(combined == 0, jnp.finfo(jnp.float32).eps, combined)
        out = jnp.log(combined)
        return feats + out.reshape(Bsz, N, C)
    x = L0_attn_x
    xn = _layernorm(x, axis=-1)
    x = x + _L0_attn_ref(xn, L0_attn_Wq, L0_attn_bq, L0_attn_Wkv, L0_attn_bkv, L0_attn_Wo, L0_attn_bo) + _L0_ffn_ref(xn, L0_ffn_A, L0_ffn_B, L0_ffn_w_gate, L0_ffn_wt_w, L0_ffn_wt_b, L0_ffn_wd_w, L0_ffn_wd_b, L0_ffn_scale)
    return x

_drawn_inputs = setup_inputs


def setup_inputs(seed=0):
    import zlib

    import numpy as np

    out = dict(_drawn_inputs(seed))
    spreads = {}
    factors = {'L0_attn_Wq': 8.0,
     'L0_attn_bq': 8.0,
     'L0_attn_Wkv': 8.0,
     'L0_attn_bkv': 8.0,
     'L0_attn_Wo': 8.0,
     'L0_attn_bo': 5.436,
     'L0_ffn_A': 8.0,
     'L0_ffn_B': 8.0,
     'L0_ffn_w_gate': 8.0,
     'L0_ffn_wt_w': 8.0,
     'L0_ffn_wt_b': 8.0,
     'L0_ffn_wd_w': 8.0,
     'L0_ffn_wd_b': 8.0}
    for name, (base, spread) in spreads.items():
        noise = np.random.default_rng([zlib.crc32(name.encode()), seed]).standard_normal(out[name].shape)
        drawn = base * np.exp(spread * noise) if base else spread * noise
        out[name] = jnp.asarray(drawn.astype(out[name].dtype))
    for name, factor in factors.items():
        out[name] = (out[name] * factor).astype(out[name].dtype)
    return out
```

```python
from contextlib import ExitStack

import concourse.bass as bass
from concourse import mybir

F32 = mybir.dt.float32
BF16 = mybir.dt.bfloat16
ALU = mybir.AluOpType
ACT = mybir.ActivationFunctionType
AX = mybir.AxisListType.X

NB = 16
T = 512
C = 256
H = 16
D = 16
NE = 6
NL = 100
NR = 16
ER = NE * NR
WC = C + 2 * D + NE + ER
KV0, G0, U0 = C, C + 2 * D, C + 2 * D + NE
LN_EPS = 1e-5
F32_EPS = 1.1920928955078125e-07
PR = 12
LB = 28
LP = 6


class Plan:

    def __init__(self):
        self.items = {e: [] for e in ("pe", "act", "dve", "pool", "sp")}
        self.seq = 0
        self.slot = 0.0
        self.log = []

    def at(self, engine, slot, fn):
        self.seq += 1
        self.items[engine].append((slot, self.seq, fn))

    def emit(self, engine, e):
        done = {}
        for slot, _, fn in sorted(self.items[engine], key=lambda t: t[:2]):
            self.slot = slot
            fn(Queue(e, done, self, engine))


class Queue:

    def __init__(self, e, done, plan, name):
        self.e, self.done, self.plan, self.name = e, done, plan, name

    def wait(self, sem, value):
        if value > self.done.get(id(sem), 0):
            self.done[id(sem)] = value
            self.plan.log.append(("w", self.name, self.plan.slot, sem, value))
            self.e.wait_ge(sem, value)

    def inc(self, ins, sem, n=1):
        self.plan.log.append(("i", self.name, self.plan.slot, sem, n))
        ins.then_inc(sem, n)


def build(nc, x, wcat, wqT, woT, wtT, wtb, bq, bkv, bo, wdb, As, Am, scale, out):
    plan = Plan()
    at = plan.at
    ctx = ExitStack()
    with ctx:
        def sb(name, shape, dt=F32):
            return ctx.enter_context(nc.sbuf_tensor(name, shape, dt))

        def ps(name):
            return ctx.enter_context(nc.psum_tensor(name, [128, 512], F32))

        sems = {}

        def S(name):
            if name not in sems:
                sems[name] = ctx.enter_context(nc.semaphore("s_" + name))
            return sems[name]

        X = sb("X", [128, 2, 4, C])
        XN = sb("XN", [128, 2, 4, C])
        Rs = sb("Rs", [128, 4, 4, C])
        st = sb("st", [128, 4, 6])
        mv = sb("mv", [128, 4, 2])
        ve = sb("ve", [128, 4])
        lv = sb("lv", [128, 4])
        y0 = sb("y0", [128, 4])
        y2 = sb("y2", [128, 4])
        y3 = sb("y3", [128, 4])
        y4 = sb("y4", [128, 4])
        rstd = sb("rstd", [128, 4])
        xT = sb("xT", [128, 2, T])
        Jt = sb("Jt", [128, 4, WC])
        Qp = sb("Qp", [128, 2, 3, T], BF16)
        q1 = sb("q1", [128, 2, T])
        Q6 = sb("Q6", [128, 2, H, T], BF16)
        VK = sb("VK", [128, 3, 4, 48])
        K6t = sb("K6t", [128, 4, 96], BF16)
        k1 = sb("k1", [128, 4, 16])
        K6 = sb("K6", [128, 3, T], BF16)
        Um = sb("Um", [128, 4, ER])
        mk = sb("mk", [128, 4, ER], BF16)
        UT = sb("UT", [128, T])
        mkT = sb("mkT", [128, T], BF16)
        gmx = sb("gmx", [128, 4])
        geq = sb("geq", [128, 4, NE])
        gw = sb("gw", [128, 4, NE])
        gm2 = sb("gm2", [128, 4])
        oh = sb("oh", [128, 4, NE])
        smx = sb("smx", [128, 4])
        Sd = sb("Sd", [128, 4, NL])
        Es = sb("Es", [128, 4, NL])
        sL = sb("sL", [128, 4])
        sR = sb("sR", [128, 4])
        En = sb("En", [128, 4, NL])
        PT = sb("PT", [128, T])
        MmT = sb("MmT", [128, T])
        Z = sb("Z", [128, 4, C])
        Cx = sb("Cx", [128, 4, C])
        Cz = sb("Cz", [128, 4, C])
        P = sb("P", [128, PR, T])
        M = sb("M", [128, 2, H])
        M1 = sb("M1", [128, 2, H])
        M3 = sb("M3", [128, 3, H], BF16)
        MT = sb("MT", [48, 2, 128], BF16)
        OTr = sb("OTr", [128, 2, T])
        Op = sb("Op", [128, T])
        Lb = sb("Lb", [128, T])
        Ln1 = sb("Ln1", [128, T])
        Ly = sb("Ly", [128, T])
        On = sb("On", [128, 2, T])
        OUT = sb("OUT", [128, 2, 2, C])
        wc = sb("wc", [128, 2, WC])
        wq = sb("wq", [128, 2, C])
        wo = sb("wo", [128, 2, C])
        wt = sb("wt", [128, 2, C])
        BW = sb("BW", [128, 2, ER + 1])
        W2 = sb("W2", [128, C])
        As_s = sb("As_s", [ER, NL])
        Am_s = sb("Am_s", [128, ER + 1])
        bq_s = sb("bq_s", [128, 2])
        bkv_s = sb("bkv_s", [128, 2 * D])
        bo_s = sb("bo_s", [128, C])
        sc_s = sb("sc_s", [128, 1])
        idf = sb("idf", [128, 128])
        idb = sb("idb", [128, 128], BF16)
        prio = sb("prio", [128, NE])

        pA = [ps("pA0"), ps("pA1")]
        pB = [ps("pB0"), ps("pB1")]
        pO = [ps("pO0"), ps("pO1")]
        pM = [ps("pM0"), ps("pM1")]

        qd = nc.dram_tensor("q_pieces", (2, 3, H, D, T), BF16, kind="Internal").ap()
        od = nc.dram_tensor("o_parts", (2, 2, 32, 8, T), F32, kind="Internal").ap()

        def bc(ap, n):
            return ap.unsqueeze(len(ap.shape)).to_broadcast(list(ap.shape) + [n])

        jobs = []

        def misc(slot, fn, release, rslot):
            job = {"slot": slot, "fn": fn, "release": release, "rslot": rslot}
            jobs.append(job)
            return job

        def setup_loads(q):
            for name, dst, src in (
                ("x0", X[:, 0, :, :], x[0].rearrange("(i p) c -> p i c", p=128)),
                ("wc", wc[:, :, :], wcat.rearrange("(c p) n -> p c n", p=128)),
                ("wt", wt[:, :, :], wtT.rearrange("(c p) n -> p c n", p=128)),
                ("wtb", BW[:, :, ER], wtb.rearrange("(c p) -> p c", p=128)),
                ("wq", wq[:, :, :], wqT.rearrange("(c p) n -> p c n", p=128)),
                ("bq", bq_s[:, :], bq.rearrange("(c p) -> p c", p=128)),
                ("bkv", bkv_s[:, :], bkv.partition_broadcast(128)),
                ("bo", bo_s[:, :], bo.partition_broadcast(128)),
                ("scale", sc_s[:, :], scale.partition_broadcast(128)),
                ("As", As_s[:, :], As),
                ("wdb", W2[ER + 1:ER + 2, :], wdb.rearrange("(a n) -> a n", a=1)),
                ("wo", wo[:, :, :], woT.rearrange("(c p) n -> p c n", p=128)),
            ):
                q.inc(q.e.dma_start(dst, src, allow_slow_non_contiguous=name in ("wtb", "bq")),
                      S(name if name != "x0" else "x_0"), 16)
            q.wait(S("am0"), 1)
            q.inc(q.e.dma_start(Am_s[1:NL, 0:ER], Am[1:NL, :]), S("am"), 16)
        at("sp", -200, setup_loads)

        def setup_pool(q):
            q.inc(q.e.memset(idf[:, :], 0.0), S("id"))
            q.inc(q.e.memset(idb[:, :], 0.0), S("id"))
            q.wait(S("id"), 2)
            for m in (idf, idb):
                q.inc(q.e.affine_select(out=m[:, :], in_=m[:, :], compare_op=ALU.not_equal, fill=1.0,
                                        base=0, pattern=[[-1, 128]], channel_multiplier=1), S("id"))
        at("pool", -200, setup_pool)

        def setup_dve(q):
            q.inc(q.e.memset(Am_s[:, :], 1.0), S("amd"))
            q.wait(S("amd"), 1)
            q.inc(q.e.memset(Am_s[0:1, :], 0.0), S("am0"))
            q.inc(q.e.memset(K6[96:128, :, :], 1.0), S("ones"))
            q.inc(q.e.memset(VK[:, :, :, 32:48], 1.0), S("ones"))
            q.inc(q.e.memset(mkT[96:128, :], 1.0), S("ones"))
            q.inc(q.e.memset(MmT[96:128, :], 1.0), S("ones"))
            for e in range(NE):
                q.inc(q.e.memset(prio[:, e:e + 1], float(NE - e)), S("prio"))
        at("dve", -200, setup_dve)

        def scale_wq(q):
            q.wait(S("wq"), 16)
            q.wait(S("bq"), 16)
            q.inc(q.e.mul(wq[:, :, :], wq[:, :, :], D ** -0.5), S("wqs"))
            q.inc(q.e.mul(bq_s[:, :], bq_s[:, :], D ** -0.5), S("wqs"))
        at("act", -100, scale_wq)

        for h in range(2):
            def bw(q, bank, h=h):
                q.wait(S("wc"), 16)
                q.wait(S("wt"), 16)
                for c in range(2):
                    mm = q.e.matmul(bank[:, 0:ER], wt[:, c, 128 * h:128 * h + 128], wc[:, c, U0:WC],
                                    start=(c == 0), stop=(c == 1))
                q.inc(mm, S("bw"))
            job = misc(-150 + h, bw, (S("bwe"), h + 1), -148)

            def bwe(q, h=h, job=job):
                q.wait(S("bw"), h + 1)
                q.inc(q.e.copy(BW[:, h, 0:ER], job["bank"][:, 0:ER]), S("bwe"))
            at("act", -149 + h, bwe)

        def w2(q, bank):
            q.wait(S("bwe"), 2)
            q.wait(S("wtb"), 16)
            for c in range(2):
                mm = q.e.matmul(bank[0:ER + 1, 0:C], BW[:, c, :], wc[:, c, 0:C], start=(c == 0), stop=(c == 1))
            q.inc(mm, S("w2"))
        job_w2 = misc(-147, w2, (S("w2e"), 1), -146)

        def w2e(q):
            q.wait(S("w2"), 1)
            q.inc(q.e.copy(W2[0:ER + 1, :], job_w2["bank"][0:ER + 1, 0:C]), S("w2e"))
        at("act", -146, w2e)

        def before(b):
            t0 = 64 * (b - 1)
            xb, r = b % 2, b % 4
            n = b + 1

            def load(q):
                q.wait(S("xn"), n - 2)
                q.wait(S("r0"), n - 2)
                q.inc(q.e.dma_start(X[:, xb, :, :], x[b].rearrange("(i p) c -> p i c", p=128)), S(f"x_{xb}"), 16)
            if b:
                at("sp", t0 - 40, load)

            def stats(q):
                q.wait(S(f"x_{xb}"), 16 * (b // 2 + 1))
                q.wait(S("mvd"), n - 1)
                for i in range(4):
                    ins = q.e.bn_stats(st[:, i, :], X[:, xb, i, :])
                q.inc(ins, S("st"))
            at("dve", t0 - 20, stats)

            def aggr(q):
                q.wait(S("st"), n)
                q.wait(S("xn"), n - 1)
                for i in range(4):
                    ins = q.e.bn_aggr(mv[:, i, :], st[:, i, :])
                q.inc(ins, S("mvd"))
            at("dve", t0 - 18, aggr)

            def var(q):
                q.wait(S("mvd"), n)
                q.wait(S("ry"), n - 1)
                q.inc(q.e.tensor_scalar(ve[:, :], mv[:, :, 1], LN_EPS, None, ALU.add), S("ve"))
            at("dve", t0 - 17, var)

            def root(q):
                q.wait(S("ve"), n)
                q.wait(S("ry"), n - 1)
                q.inc(q.e.activation(lv[:, :], ve[:, :], ACT.Ln), S("lv"))
                q.wait(S("lv"), n)
                q.inc(q.e.activation(y0[:, :], lv[:, :], ACT.Exp, scale=-0.5), S("y0"))
            at("act", t0 - 16, root)

            def refine(q):
                q.wait(S("y0"), n)
                q.inc(q.e.tensor_tensor(y2[:, :], y0[:, :], y0[:, :], ALU.mult), S("y2"))
                q.wait(S("y2"), n)
                q.inc(q.e.tensor_tensor(y3[:, :], y2[:, :], ve[:, :], ALU.mult), S("y3"))
                q.wait(S("y3"), n)
                q.inc(q.e.tensor_scalar(y4[:, :], y3[:, :], -0.5, 1.5, ALU.mult, ALU.add), S("y4"))
                q.wait(S("y4"), n)
                q.inc(q.e.tensor_tensor(rstd[:, :], y4[:, :], y0[:, :], ALU.mult), S("ry"))
            at("dve", t0 - 12, refine)

            def norm(q):
                q.wait(S("ry"), n)
                q.wait(S("xt"), 2 * (n - 2))
                q.wait(S("r0"), n - 2)
                for i in range(4):
                    ins = q.e.tensor_scalar(XN[:, xb, i, :], X[:, xb, i, :], mv[:, i, 0:1], rstd[:, i:i + 1],
                                            ALU.subtract, ALU.mult)
                q.inc(ins, S("xn"))
            at("dve", t0 - 8, norm)

            def residual(q):
                q.wait(S("xn"), n)
                q.wait(S("fo"), 2 * (n - 4))
                q.inc(q.e.tensor_tensor(Rs[:, r, :, :], X[:, xb, :, :], XN[:, xb, :, :], ALU.add), S("r0"))
                q.wait(S("r0"), n)
                q.wait(S("bo"), 16)
                q.inc(q.e.tensor_tensor(Rs[:, r, :, :], Rs[:, r, :, :],
                                        bo_s[:, :].unsqueeze(1).to_broadcast([128, 4, C]), ALU.add), S("r1"))
            at("pool", t0 + 40, residual)

            for c in range(2):
                def xt(q, bank, c=c):
                    q.wait(S("xn"), n)
                    q.wait(S("id"), 4)
                    for i in range(4):
                        mm = q.e.transpose(bank[:, 128 * i:128 * i + 128], XN[:, xb, i, 128 * c:128 * c + 128],
                                           idf[:, :])
                    q.inc(mm, S("xt"))
                job = misc(t0 + 2 * c, xt, (S("xte"), 2 * b + c + 1), t0 + 2 * c + 1)

                def xte(q, c=c, job=job):
                    q.wait(S("xt"), 2 * b + c + 1)
                    q.wait(S("j"), 4 * b)
                    q.wait(S("q"), 2 * b)
                    q.inc(q.e.copy(xT[:, c, :], job["bank"][:, :]), S("xte"))
                at("act", t0 + 2 * c + 1, xte)

            for i in range(4):
                def j(q, bank, i=i):
                    q.wait(S("xte"), 2 * b + 2)
                    q.wait(S("wc"), 16)
                    for c in range(2):
                        mm = q.e.matmul(bank[:, 0:WC], xT[:, c, 128 * i:128 * i + 128], wc[:, c, :],
                                        start=(c == 0), stop=(c == 1))
                    q.inc(mm, S("j"))
                job = misc(t0 + 5 + 3 * i, j, (S("je"), 4 * b + i + 1), t0 + 6 + 3 * i)

                def je(q, i=i, job=job):
                    q.wait(S("j"), 4 * b + i + 1)
                    if i == 0:
                        q.wait(S("z"), 2 * b)
                        q.wait(S("ul"), b)
                    q.inc(q.e.copy(Jt[:, i, :], job["bank"][:, 0:WC]), S("je"))
                at("act", t0 + 6 + 3 * i, je)

            for g in range(2):
                def qt(q, bank, g=g):
                    q.wait(S("xte"), 2 * b + 2)
                    q.wait(S("wqs"), 2)
                    for c in range(2):
                        mm = q.e.matmul(bank[:, :], wq[:, c, 128 * g:128 * g + 128], xT[:, c, :],
                                        start=(c == 0), stop=(c == 1))
                    q.inc(mm, S("q"))
                job = misc(t0 + 17 + 4 * g, qt, (S("q1"), 2 * b + g + 1), t0 + 19 + 4 * g)

                def qh(q, g=g, job=job):
                    q.wait(S("q"), 2 * b + g + 1)
                    if b:
                        q.wait(S("qw"), 32 * b)
                    q.wait(S("wqs"), 2)
                    q.inc(q.e.activation(Qp[:, g, 0, :], job["bank"][:, :], ACT.Identity, bias=bq_s[:, g:g + 1]),
                          S("qh"))
                at("act", t0 + 18 + 4 * g, qh)

                def qr(q, g=g, job=job):
                    q.wait(S("qh"), 2 * b + g + 1)
                    q.wait(S("ql"), 2 * (b - 1) + g + 1)
                    q.inc(q.e.scalar_tensor_tensor(out=q1[:, g, :], in0=job["bank"][:, :], scalar=bq_s[:, g:g + 1],
                                                   in1=Qp[:, g, 0, :], op0=ALU.add, op1=ALU.subtract), S("q1"))
                at("dve", t0 + 19 + 4 * g, qr)

                def qm(q, g=g):
                    q.wait(S("q1"), 2 * b + g + 1)
                    q.inc(q.e.tensor_copy(Qp[:, g, 1, :], q1[:, g, :]), S("qm"))
                at("dve", t0 + 20 + 4 * g, qm)

                def ql(q, g=g):
                    q.wait(S("qm"), 2 * b + g + 1)
                    q.inc(q.e.tensor_tensor(Qp[:, g, 2, :], q1[:, g, :], Qp[:, g, 1, :], ALU.subtract), S("ql"))
                at("pool", t0 + 21 + 4 * g, ql)

                def qw(q, g=g):
                    q.wait(S("ql"), 2 * b + g + 1)
                    if b >= 2:
                        q.wait(S(f"qr_{xb}"), 96 * (b // 2))
                    q.inc(q.e.dma_start(qd[xb, :, 8 * g:8 * g + 8].rearrange("p h d t -> (h d) p t"),
                                        Qp[:, g, :, :]), S("qw"), 16)
                at("sp", t0 + 22 + 4 * g, qw)

            def qread(q):
                q.wait(S("qw"), 32 * n)
                if b >= 2:
                    q.wait(S("b"), 64 * (b - 1))
                for k, piece in enumerate((0, 0, 0, 1, 1, 2)):
                    q.inc(q.e.dma_start(Q6[16 * k:16 * k + 16, xb, :, :], qd[xb, piece].rearrange("h d t -> d h t")),
                          S(f"qr_{xb}"), 16)
            at("sp", t0 + 31, qread)

            v3 = b % 3

            def kv(q):
                q.wait(S("je"), 4 * n)
                q.wait(S("bkv"), 16)
                if b >= 3:
                    q.wait(S("pv"), 16 * (b - 2))
                q.inc(q.e.tensor_tensor(VK[:, v3, :, 0:32], Jt[:, :, KV0:G0],
                                        bkv_s[:, :].unsqueeze(1).to_broadcast([128, 4, 2 * D]), ALU.add), S("kv"))
            at("dve", t0 + 16, kv)

            def ksplit(q):
                kf = VK[:, v3, :, 0:16]
                sl = [K6t[:, :, 16 * s:16 * s + 16] for s in range(6)]
                q.wait(S("kv"), n)
                q.wait(S("k6t"), n - 1)
                q.inc(q.e.tensor_copy(sl[0], kf), S("k0"))
                q.wait(S("k0"), n)
                q.inc(q.e.tensor_tensor(k1[:, :, :], kf, sl[0], ALU.subtract), S("k1"))
                q.e.tensor_copy(sl[3], sl[0])
                q.e.tensor_copy(sl[5], sl[0])
                q.wait(S("k1"), n)
                q.inc(q.e.tensor_copy(sl[1], k1[:, :, :]), S("k2"))
                q.wait(S("k2"), n)
                q.inc(q.e.tensor_tensor(sl[2], k1[:, :, :], sl[1], ALU.subtract), S("k3"))
                q.inc(q.e.tensor_copy(sl[4], sl[1]), S("k6"))
            at("dve", t0 + 17.2, ksplit)

            def kt(q, bank):
                q.wait(S("k6"), n)
                q.wait(S("id"), 4)
                o = bank[:, :].bitcast(BF16)
                for i in range(4):
                    mm = q.e.transpose(o[0:96, 128 * i:128 * i + 128], K6t[:, i, :], idb[:, :])
                q.inc(mm, S("k6t"))
            job_k = misc(t0 + 26, kt, (S("k6e"), n), t0 + 27)

            def kte(q):
                q.wait(S("k6t"), n)
                q.wait(S("ones"), 4)
                if b >= 3:
                    q.wait(S("b"), 64 * (b - 2))
                q.inc(q.e.copy(K6[0:96, v3, :], job_k["bank"][0:96, :].bitcast(BF16)[:, 0:T]), S("k6e"))
            at("act", t0 + 27, kte)

            def gate(q):
                g = Jt[:, :, G0:U0]
                q.wait(S("prio"), NE)
                q.wait(S("je"), 4 * n)
                q.inc(q.e.tensor_reduce(gmx[:, :], g, AX, ALU.max), S("g0"))
                q.wait(S("g0"), n)
                q.inc(q.e.tensor_tensor(geq[:, :, :], g, bc(gmx[:, :], NE), ALU.is_equal), S("g1"))
                q.wait(S("g1"), n)
                q.inc(q.e.tensor_tensor(gw[:, :, :], geq[:, :, :],
                                        prio[:, :].unsqueeze(1).to_broadcast([128, 4, NE]), ALU.mult), S("g2"))
                q.wait(S("g2"), n)
                q.inc(q.e.tensor_reduce(gm2[:, :], gw[:, :, :], AX, ALU.max), S("g3"))
                q.wait(S("g3"), n)
                q.wait(S("mk"), n - 1)
                q.inc(q.e.tensor_tensor(oh[:, :, :], gw[:, :, :], bc(gm2[:, :], NE), ALU.is_equal), S("oh"))
            at("dve", t0 + 24.3, gate)

            def mask(q):
                q.wait(S("oh"), n)
                q.wait(S("ut"), n - 1)
                q.wait(S("mkt"), n - 1)
                o4 = bc(oh[:, :, :], NR)
                q.inc(q.e.tensor_tensor(Um[:, :, :].rearrange("p i (e r) -> p i e r", r=NR),
                                        Jt[:, :, U0:WC].rearrange("p i (e r) -> p i e r", r=NR), o4, ALU.mult),
                      S("ul"))
                q.inc(q.e.tensor_copy(mk[:, :, :].rearrange("p i (e r) -> p i e r", r=NR), o4), S("mk"))
            at("pool", t0 + 26, mask)

            def ut(q, bank):
                q.wait(S("ul"), n)
                for i in range(4):
                    mm = q.e.transpose(bank[0:ER, 128 * i:128 * i + 128], Um[:, i, :], idf[:, :])
                q.inc(mm, S("ut"))
            job_u = misc(t0 + 30, ut, (S("ute"), n), t0 + 31)

            def ute(q):
                q.wait(S("ut"), n)
                q.wait(S("sc"), n - 1)
                q.inc(q.e.copy(UT[0:ER, :], job_u["bank"][0:ER, :]), S("ute"))
            at("act", t0 + 31, ute)

            def mt(q, bank):
                q.wait(S("mk"), n)
                o = bank[:, :].bitcast(BF16)
                for i in range(4):
                    mm = q.e.transpose(o[0:ER, 128 * i:128 * i + 128], mk[:, i, :], idb[:, :])
                q.inc(mm, S("mkt"))
            job_m = misc(t0 + 32, mt, (S("mke"), n), t0 + 33)

            def mke(q):
                q.wait(S("mkt"), n)
                q.wait(S("mm"), n - 1)
                q.inc(q.e.copy(mkT[0:ER, :], job_m["bank"][0:ER, :].bitcast(BF16)[:, 0:T]), S("mke"))
            at("act", t0 + 33, mke)

            def sc(q, bank):
                q.wait(S("ute"), n)
                q.wait(S("As"), 16)
                for i in range(4):
                    mm = q.e.matmul(bank[:, NL * i:NL * i + NL], UT[0:ER, 128 * i:128 * i + 128], As_s[:, :],
                                    start=True, stop=True)
                q.inc(mm, S("sc"))
            job_s = misc(t0 + 36, sc, (S("sd"), n), t0 + 39)

            def smax(q):
                v = job_s["bank"][:, 0:4 * NL].rearrange("p (i l) -> p i l", l=NL)
                q.wait(S("sc"), n)
                q.inc(q.e.tensor_reduce(smx[:, :], v, AX, ALU.max), S("sm"))
                q.wait(S("sm"), n)
                q.wait(S("es"), n - 1)
                q.inc(q.e.tensor_tensor(Sd[:, :, :], v, bc(smx[:, :], NL), ALU.subtract), S("sd"))
            at("dve", t0 + 38.2, smax)

            def sexp(q):
                q.wait(S("sd"), n)
                q.wait(S("en"), n - 1)
                q.inc(q.e.activation(Es[:, :, :], Sd[:, :, :], ACT.Exp, scale=C ** -0.5), S("es"))
            at("act", t0 + 39.5, sexp)

            def ssum(q):
                q.wait(S("es"), n)
                q.inc(q.e.tensor_reduce(sL[:, :], Es[:, :, :], AX, ALU.add), S("sl"))
                q.wait(S("sl"), n)
                q.wait(S("en"), n - 1)
                q.inc(q.e.reciprocal(sR[:, :], sL[:, :]), S("sr"))
            at("dve", t0 + 40.2, ssum)

            def snorm(q):
                q.wait(S("sr"), n)
                q.wait(S("pt"), n - 1)
                q.inc(q.e.tensor_tensor(En[:, :, :], Es[:, :, :], bc(sR[:, :], NL), ALU.mult), S("en"))
            at("pool", t0 + 41, snorm)

            def pt(q, bank):
                q.wait(S("en"), n)
                for i in range(4):
                    mm = q.e.transpose(bank[0:NL, 128 * i:128 * i + 128], En[:, i, :], idf[:, :])
                q.inc(mm, S("pt"))
            job_p = misc(t0 + 44, pt, (S("pte"), n), t0 + 45)

            def pte(q):
                q.wait(S("pt"), n)
                q.wait(S("ma"), n - 1)
                q.inc(q.e.copy(PT[0:NL, :], job_p["bank"][0:NL, :]), S("pte"))
            at("act", t0 + 45, pte)

            def ma(q, bank):
                q.wait(S("pte"), n)
                q.wait(S("am"), 16)
                q.inc(q.e.matmul(bank[0:ER + 1, :], Am_s[0:NL, :], PT[0:NL, :], start=True, stop=True), S("ma"))
            job_a = misc(t0 + 48, ma, (S("mm"), n), t0 + 49)

            def mm_(q):
                q.wait(S("ma"), n)
                q.wait(S("mke"), n)
                q.wait(S("ones"), 4)
                q.wait(S("d"), 2 * (n - 1))
                q.inc(q.e.tensor_tensor(MmT[0:ER + 1, :], job_a["bank"][0:ER + 1, :], mkT[0:ER + 1, :], ALU.mult),
                      S("mm"))
            at("dve", t0 + 49, mm_)

            for k in range(2):
                def dd(q, bank, k=k):
                    q.wait(S("mm"), n)
                    q.wait(S("w2e"), 1)
                    q.wait(S("wdb"), 16)
                    for i in range(2):
                        t = 2 * k + i
                        mm = q.e.matmul(bank[:, C * i:C * i + C], MmT[0:ER + 2, 128 * t:128 * t + 128],
                                        W2[0:ER + 2, :], start=True, stop=True)
                    q.inc(mm, S("d"))
                job = misc(t0 + 51.6 + 2 * k, dd, (S("z"), 2 * b + k + 1), t0 + 52.6 + 2 * k)

                def zz(q, k=k, job=job):
                    q.wait(S("d"), 2 * b + k + 1)
                    q.wait(S("cx"), n - 1)
                    q.wait(S("je"), 4 * n)
                    q.inc(q.e.tensor_tensor(Z[:, 2 * k:2 * k + 2, :],
                                            job["bank"][:, :].rearrange("p (i c) -> p i c", i=2),
                                            Jt[:, 2 * k:2 * k + 2, 0:C], ALU.add), S("z"))
                at("dve", t0 + 52.6 + 2 * k, zz)

            def dexp(q):
                q.wait(S("z"), 2 * n)
                q.wait(S("scale"), 16)
                q.wait(S("lg"), n - 1)
                q.inc(q.e.activation(Cx[:, :, :], Z[:, :, :], ACT.Exp, scale=sc_s[:, 0:1]), S("cx"))
            at("act", t0 + 56, dexp)

            def guard(q):
                q.wait(S("cx"), n)
                q.inc(q.e.tensor_scalar(Cz[:, :, :], Cx[:, :, :], 0.0, F32_EPS, ALU.is_equal, ALU.mult), S("c0"))
                q.wait(S("c0"), n)
                q.inc(q.e.tensor_tensor(Cx[:, :, :], Cx[:, :, :], Cz[:, :, :], ALU.add), S("c1"))
            at("pool", t0 + 57, guard)

            def dlog(q):
                q.wait(S("c1"), n)
                q.wait(S("r2"), n - 1)
                q.inc(q.e.activation(Cz[:, :, :], Cx[:, :, :], ACT.Ln), S("lg"))
            at("act", t0 + 65, dlog)

            def radd(q):
                q.wait(S("lg"), n)
                q.wait(S("r1"), n)
                q.inc(q.e.tensor_tensor(Rs[:, r, :, :], Rs[:, r, :, :], Cz[:, :, :], ALU.add), S("r2"))
            at("pool", t0 + 66, radd)

        for b in range(NB):
            before(b)

        for n in range(64 * NB):
            b, qq, h = n // 64, n % 64 // 16, n % 16
            g = n // 16

            def a(q, n=n, b=b, qq=qq, h=h):
                if n % 64 == 0:
                    q.wait(S(f"qr_{b % 2}"), 96 * (b // 2 + 1))
                    q.wait(S("k6e"), b + 1)
                q.wait(S("mx"), n - 1)
                q.inc(q.e.matmul(pA[n % 2][:, :], Q6[0:96, b % 2, h, 128 * qq:128 * qq + 128],
                                 K6[0:96, b % 3, :], start=True, stop=True), S("a"))
            at("pe", n, a)

            def mx(q, n=n, g=g, h=h):
                q.wait(S("a"), n + 1)
                q.wait(S("m0"), 2 * (g - 1))
                q.inc(q.e.tensor_reduce(M[:, g % 2, h:h + 1], pA[n % 2][:, :], AX, ALU.max, negate=True), S("mx"))
            at("dve", n + 0.5, mx)

        for g in range(4 * NB):
            b, qq = g // 4, g % 4
            t1 = 16 * g + 16
            mg = M[:, g % 2, :]

            def ms(q, g=g, mg=mg):
                m1 = M1[:, g % 2, :]
                q.wait(S("mx"), 16 * g + 16)
                q.wait(S("mt"), g)
                q.inc(q.e.tensor_copy(M3[:, 0, :], mg), S("mh"))
                q.wait(S("mh"), g + 1)
                q.inc(q.e.tensor_tensor(m1, mg, M3[:, 0, :], ALU.subtract), S("m0"))
                q.wait(S("m0"), 2 * g + 1)
                q.inc(q.e.tensor_copy(M3[:, 1, :], m1), S("mm1"))
                q.wait(S("mm1"), g + 1)
                q.inc(q.e.tensor_tensor(M3[:, 2, :], m1, M3[:, 1, :], ALU.subtract), S("m0"))
            at("dve", t1 - 0.3, ms)

            def mtp(q, bank, g=g):
                q.wait(S("m0"), 2 * g + 2)
                q.wait(S("id"), 4)
                q.inc(q.e.transpose(bank[:, :].bitcast(BF16)[0:48, 0:128],
                                    M3[:, :, :].rearrange("p k h -> p (k h)"), idb[:, :]), S("mt"))
            job = misc(t1 + 1.2, mtp, (S("mte"), g + 1), t1 + 2)

            def mte(q, g=g, job=job):
                q.wait(S("mt"), g + 1)
                if g >= 2:
                    q.wait(S(f"md_{g % 2}"), 48 * (g // 2))
                q.inc(q.e.copy(MT[:, g % 2, :], job["bank"][0:48, :].bitcast(BF16)[:, 0:128]), S("mte"))
            at("act", t1 + 2, mte)

            def md(q, g=g, b=b, qq=qq):
                q.wait(S("mte"), g + 1)
                if b >= 2:
                    q.wait(S("b"), 64 * (b - 1))
                for k in range(3):
                    q.inc(q.e.dma_start(Q6[96 + k:97 + k, b % 2, :, 128 * qq:128 * qq + 128],
                                        MT[16 * k:16 * k + 16, g % 2, :]), S(f"md_{g % 2}"), 16)
            at("sp", t1 + 3, md)

        for u in range(64 * NB):
            b, g, i, j = u // 64, u % 64 // 16, u % 16 // 4, u % 4
            gg = u // 16

            def bs(q, u=u, b=b, i=i, j=j, g=g, gg=gg):
                if u % 16 == 0:
                    q.wait(S(f"md_{gg % 2}"), 48 * (gg // 2 + 1))
                q.wait(S("e"), u - 1)
                hh = 4 * g + j
                q.inc(q.e.matmul(pB[u % 2][:, :], K6[0:99, b % 3, 128 * i:128 * i + 128],
                                 Q6[0:99, b % 2, :, 32 * hh:32 * hh + 32], start=True, stop=True), S("b"))
            at("pe", u + LB + 0.3, bs)

            def ex(q, u=u):
                q.wait(S("b"), u + 1)
                if u >= PR:
                    q.wait(S("pv"), (u - PR) // 4 + 1)
                q.inc(q.e.activation(P[:, u % PR, :], pB[u % 2][:, :], ACT.Exp), S("e"))
            at("act", u + LB + 0.6, ex)

        for w in range(16 * NB):
            b, g, i = w // 16, w % 16 // 4, w % 4
            gg = w // 4

            def pv(q, w=w, b=b, i=i, gg=gg):
                q.wait(S("e"), 4 * w + 4)
                q.wait(S("kv"), b + 1)
                q.wait(S("ones"), 4)
                if i == 0:
                    q.wait(S("ot"), gg - 1)
                for j in range(4):
                    mm = q.e.matmul(pO[gg % 2][32 * j:32 * j + 32, :], VK[:, b % 3, i, 16:48],
                                    P[:, (4 * w + j) % PR, :], start=(i == 0), stop=(i == 3))
                q.inc(mm, S("pv"))
            at("pe", 4 * w + LB + LP, pv)

        for gg in range(4 * NB):
            b, g = gg // 4, gg % 4
            t2 = 16 * gg + LB + LP + 12
            hf = g // 2
            nh = 2 * b + hf

            def ot(q, gg=gg):
                q.wait(S("pv"), 4 * gg + 4)
                if gg >= 2:
                    q.wait(S(f"ow_{gg % 2}"), 64 * (gg // 2))
                q.inc(q.e.copy(OTr[:, gg % 2, :], pO[gg % 2][:, :]), S("ot"))
            at("act", t2 + 1, ot)

            def ow(q, gg=gg, b=b, g=g, hf=hf):
                q.wait(S("ot"), gg + 1)
                if b >= 2:
                    q.wait(S("or"), 32 * (2 * (b - 2) + hf + 1))
                for j in range(4):
                    q.inc(q.e.dma_start(od[b % 2, hf, :, 4 * (g % 2) + j, :], OTr[32 * j:32 * j + 32, gg % 2, :]),
                          S(f"ow_{gg % 2}"), 16)
            at("sp", t2 + 2, ow)

            if g % 2 == 0:
                continue

            def orr(q, nh=nh, b=b, hf=hf, gg=gg):
                q.wait(S("ow_0"), 64 * (nh + 1))
                q.wait(S("ow_1"), 64 * (nh + 1))
                q.wait(S("on"), nh)
                v = od[b % 2, hf].rearrange("r h t -> (r h) t")
                q.inc(q.e.dma_start(Lb[:, :], v[128:256, :]), S("or"), 16)
                q.inc(q.e.dma_start(Op[:, :], v[0:128, :]), S("or"), 16)
            at("sp", t2 + 6, orr)

            def lr(q, nh=nh):
                q.wait(S("or"), 32 * (nh + 1))
                q.wait(S("o0"), nh)
                q.inc(q.e.activation(Ln1[:, :], Lb[:, :], ACT.Ln), S("l0"))
                q.wait(S("l0"), nh + 1)
                q.wait(S("on"), nh)
                q.inc(q.e.activation(Ly[:, :], Ln1[:, :], ACT.Exp, scale=-1.0), S("l1"))
            at("act", t2 + 9, lr)

            def on(q, nh=nh, b=b, hf=hf):
                q.wait(S("l1"), nh + 1)
                q.inc(q.e.tensor_tensor(Ln1[:, :], Lb[:, :], Ly[:, :], ALU.mult), S("n0"))
                q.wait(S("n0"), nh + 1)
                q.inc(q.e.tensor_scalar(Ln1[:, :], Ln1[:, :], -1.0, 2.0, ALU.mult, ALU.add), S("n1"))
                q.wait(S("n1"), nh + 1)
                q.inc(q.e.tensor_tensor(Ln1[:, :], Ln1[:, :], Ly[:, :], ALU.mult), S("o0"))
                q.wait(S("o0"), nh + 1)
                q.wait(S("fo"), 2 * b)
                q.inc(q.e.tensor_tensor(On[:, hf, :].rearrange("p (t h) -> p h t", h=H),
                                        Op[:, :].rearrange("p (h t) -> p h t", h=H),
                                        Ln1[:, :].rearrange("p (h t) -> p h t", h=H), ALU.mult), S("on"))
            at("pool", t2 + 10, on)

        for b in range(NB):
            t3 = 64 * b + 64 + LB + 28
            for k in range(2):
                def oo(q, bank, b=b, k=k):
                    q.wait(S("on"), 2 * b + 2)
                    q.wait(S("wo"), 16)
                    for i in range(2):
                        t = 2 * k + i
                        for c in range(2):
                            mm = q.e.matmul(bank[:, C * i:C * i + C], On[:, c, 128 * t:128 * t + 128], wo[:, c, :],
                                            start=(c == 0), stop=(c == 1))
                    q.inc(mm, S("o"))
                job = misc(t3 + 2 * k, oo, (S("fo"), 2 * b + k + 1), t3 + 2 * k + 1.6)

                def fo(q, b=b, k=k, job=job):
                    m = 2 * b + k
                    q.wait(S("o"), m + 1)
                    q.wait(S("r2"), b + 1)
                    if m >= 2:
                        q.wait(S(f"st_{k}"), 16 * b)
                    q.inc(q.e.tensor_tensor(OUT[:, k, :, :], job["bank"][:, :].rearrange("p (i c) -> p i c", i=2),
                                            Rs[:, b % 4, 2 * k:2 * k + 2, :], ALU.add), S("fo"))
                at("dve", t3 + 2 * k + 1.6, fo)

                def store(q, b=b, k=k):
                    q.wait(S("fo"), 2 * b + k + 1)
                    q.inc(q.e.dma_start(out[b, 256 * k:256 * k + 256, :].rearrange("(i p) c -> p i c", p=128),
                                        OUT[:, k, :, :]), S(f"st_{k}"), 16)
                at("sp", t3 + 2 * k + 3, store)

        def finish(q):
            for k in range(2):
                q.wait(S(f"st_{k}"), 16 * NB)
            for k in range(2):
                q.wait(S(f"qr_{k}"), 96 * (NB // 2))
                q.wait(S(f"ow_{k}"), 64 * 2 * NB)
        at("sp", 1e9, finish)

        jobs.sort(key=lambda j: j["slot"])
        for n, job in enumerate(jobs):
            job["bank"] = pM[n % 2]
            if n >= 2:
                assert jobs[n - 2]["rslot"] <= job["slot"], (n, jobs[n - 2]["slot"], job["slot"])

            def run(q, n=n, job=job):
                if n >= 2:
                    q.wait(*jobs[n - 2]["release"])
                job["fn"](q, job["bank"])
            at("pe", job["slot"] + 0.15, run)

        block = ctx.enter_context(nc.Block())

        @block.tensor
        def _(e):
            plan.emit("pe", e)

        @block.scalar
        def _(e):
            plan.emit("act", e)

        @block.vector
        def _(e):
            plan.emit("dve", e)

        @block.gpsimd
        def _(e):
            plan.emit("pool", e)

        @block.sync
        def _(e):
            plan.emit("sp", e)

    return plan


def kernel(**inputs):
    import numpy as np
    import concourse.bacc as bacc
    from concourse.bass_utils import run_bass_kernel_spmd

    a = {k: np.asarray(v) for k, v in inputs.items()}
    AA, BB = a["L0_ffn_A"], a["L0_ffn_B"]
    arrays = {
        "x": a["L0_attn_x"],
        "wcat": np.concatenate([a["L0_ffn_wd_w"].T, a["L0_attn_Wkv"].T, a["L0_ffn_w_gate"],
                                BB.reshape(ER, C).T], axis=1),
        "wqT": a["L0_attn_Wq"].T,
        "woT": a["L0_attn_Wo"].T.reshape(2, 8, D, C).transpose(0, 2, 1, 3).reshape(C, C),
        "wtT": a["L0_ffn_wt_w"].T,
        "wtb": a["L0_ffn_wt_b"],
        "bq": a["L0_attn_bq"],
        "bkv": a["L0_attn_bkv"],
        "bo": a["L0_attn_bo"],
        "wdb": a["L0_ffn_wd_b"],
        "As": AA.transpose(0, 2, 1).reshape(ER, NL),
        "Am": AA.transpose(1, 0, 2).reshape(NL, ER),
        "scale": a["L0_ffn_scale"],
    }
    nc = bacc.Bacc("TRN2", target_bir_lowering=False, num_devices=1)
    args, feed = [], {}
    for name, v in arrays.items():
        v = np.ascontiguousarray(v)
        feed[f"in_{name}"] = v
        args.append(nc.dram_tensor(f"in_{name}", v.shape, mybir.dt.from_np(v.dtype), kind="ExternalInput").ap())
    o = nc.dram_tensor("out_0", (NB, T, C), F32, kind="ExternalOutput").ap()
    build(nc, *args, o)
    r = run_bass_kernel_spmd(nc, [feed], core_ids=[0])
    return r.results[0]["out_0"]
```

```python
from contextlib import ExitStack

import concourse.bass as bass
from concourse import mybir

F32 = mybir.dt.float32
BF16 = mybir.dt.bfloat16
F32R = mybir.dt.float32r
ALU = mybir.AluOpType
ACT = mybir.ActivationFunctionType
AX = mybir.AxisListType.X

NB = 16
T = 512
C = 256
H = 16
D = 16
NE = 6
NL = 100
NR = 16
ER = NE * NR
WC = C + 2 * D + NE + ER
KV0, G0, U0 = C, C + 2 * D, C + 2 * D + NE
LN_EPS = 1e-5
F32_EPS = 1.1920928955078125e-07
PR = 12
LB = 30
LP = 7

S_XT = (7, 8)
S_J = ((14, 15), (20, 22), (23, 24), (26, 27))
S_Q = ((30, 31), (38, 39))
S_K, S_U, S_MK, S_SC, S_PT, S_MA = 36, 42, 44, 46, 56, 63
S_D = ((68, 70), (74, 75))
S_O = ((122, 123), (124, 126))


class Plan:

    def __init__(self):
        self.items = {e: [] for e in ("pe", "act", "dve", "pool", "sp")}
        self.seq = 0
        self.slot = 0.0
        self.log = []

    def at(self, engine, slot, fn):
        self.seq += 1
        self.items[engine].append((slot, self.seq, fn))

    def emit(self, engine, e):
        done = {}
        for slot, _, fn in sorted(self.items[engine], key=lambda t: t[:2]):
            self.slot = slot
            fn(Queue(e, done, self, engine))


class Queue:

    def __init__(self, e, done, plan, name):
        self.e, self.done, self.plan, self.name = e, done, plan, name

    def wait(self, sem, value):
        if value > self.done.get(id(sem), 0):
            self.done[id(sem)] = value
            self.plan.log.append(("w", self.name, self.plan.slot, sem, value))
            self.e.wait_ge(sem, value)

    def inc(self, ins, sem, n=1):
        self.plan.log.append(("i", self.name, self.plan.slot, sem, n))
        ins.then_inc(sem, n)


def build(nc, x, wcat, wqT, woT, wtT, wtb, bq, bkv, bo, wdb, As, Am, scale, out):
    plan = Plan()
    at = plan.at
    ctx = ExitStack()
    with ctx:
        def sb(name, shape, dt=F32):
            return ctx.enter_context(nc.sbuf_tensor(name, shape, dt))

        def ps(name):
            return ctx.enter_context(nc.psum_tensor(name, [128, 512], F32))

        sems = {}

        def S(name):
            if name not in sems:
                sems[name] = ctx.enter_context(nc.semaphore("s_" + name))
            return sems[name]

        X = sb("X", [128, 2, 4, C])
        XN = sb("XN", [128, 2, 4, C])
        Rs = sb("Rs", [128, 4, 4, C])
        st = sb("st", [128, 4, 6])
        mv = sb("mv", [128, 4, 2])
        ve = sb("ve", [128, 4])
        lv = sb("lv", [128, 4])
        y0 = sb("y0", [128, 4])
        y2 = sb("y2", [128, 4])
        y3 = sb("y3", [128, 4])
        y4 = sb("y4", [128, 4])
        rstd = sb("rstd", [128, 4])
        xT = sb("xT", [128, 2, 2, T], F32R)
        wcr = sb("wcr", [128, 2, 2, WC], F32R)
        wqr = sb("wqr", [128, 2, 2, C], F32R)
        wor = sb("wor", [128, 2, 2, C], F32R)
        Jt = sb("Jt", [128, 4, WC])
        Qp = sb("Qp", [128, 2, 3, T], BF16)
        q1 = sb("q1", [128, 2, T])
        Q6 = sb("Q6", [128, 2, H, T], BF16)
        VK = sb("VK", [128, 3, 4, 48])
        K6t = sb("K6t", [128, 4, 96], BF16)
        k1 = sb("k1", [128, 4, 16])
        K6 = sb("K6", [128, 3, T], BF16)
        Um = sb("Um", [128, 4, ER])
        mk = sb("mk", [128, 4, ER], BF16)
        UT = sb("UT", [128, T])
        mkT = sb("mkT", [128, T], BF16)
        gmx = sb("gmx", [128, 4])
        geq = sb("geq", [128, 4, NE])
        gw = sb("gw", [128, 4, NE])
        gm2 = sb("gm2", [128, 4])
        oh = sb("oh", [128, 4, NE])
        smx = sb("smx", [128, 4])
        Sd = sb("Sd", [128, 4, NL])
        Es = sb("Es", [128, 4, NL])
        sL = sb("sL", [128, 4])
        sR = sb("sR", [128, 4])
        En = sb("En", [128, 4, NL])
        PT = sb("PT", [128, T])
        MmT = sb("MmT", [128, T])
        Z = sb("Z", [128, 4, C])
        Cx = sb("Cx", [128, 4, C])
        Cz = sb("Cz", [128, 4, C])
        P = sb("P", [128, PR, T])
        M = sb("M", [128, 2, H])
        M1 = sb("M1", [128, 2, H])
        M3 = sb("M3", [128, 3, H], BF16)
        MT = sb("MT", [48, 2, 128], BF16)
        OTr = sb("OTr", [128, 2, T])
        Op = sb("Op", [128, T])
        Lb = sb("Lb", [128, T])
        Ln1 = sb("Ln1", [128, T])
        Ly = sb("Ly", [128, T])
        Ov = sb("Ov", [128, T])
        On = sb("On", [128, 2, 2, T], F32R)
        OUT = sb("OUT", [128, 2, 2, C])
        wc = sb("wc", [128, 2, WC])
        wq = sb("wq", [128, 2, C])
        wo = sb("wo", [128, 2, C])
        wt = sb("wt", [128, 2, C])
        BW = sb("BW", [128, 2, ER + 1])
        W2 = sb("W2", [128, C])
        As_s = sb("As_s", [ER, NL])
        Am_s = sb("Am_s", [128, ER + 1])
        bq_s = sb("bq_s", [128, 2])
        bkv_s = sb("bkv_s", [128, 2 * D])
        bo_s = sb("bo_s", [128, C])
        sc_s = sb("sc_s", [128, 1])
        idf = sb("idf", [128, 128])
        idb = sb("idb", [128, 128], BF16)
        prio = sb("prio", [128, NE])

        pA = [ps("pA0"), ps("pA1")]
        pB = [ps("pB0"), ps("pB1")]
        pO = [ps("pO0"), ps("pO1")]
        pM = [ps("pM0"), ps("pM1")]

        qd = nc.dram_tensor("q_pieces", (2, 3, H, D, T), BF16, kind="Internal").ap()
        od = nc.dram_tensor("o_parts", (2, 2, 32, 8, T), F32, kind="Internal").ap()

        def bc(ap, n):
            return ap.unsqueeze(len(ap.shape)).to_broadcast(list(ap.shape) + [n])

        jobs = []

        def misc(slots, fn, release, rslot):
            slots = slots if isinstance(slots, tuple) else (slots,)
            job = {"slots": slots, "fn": fn, "release": release, "rslot": rslot}
            jobs.append(job)
            return job

        def chain(engine, slot, step, steps):
            for n, fn in enumerate(steps):
                at(engine, slot + step * n, fn)

        def setup_loads(q):
            for name, dst, src in (
                ("x0", X[:, 0, :, :], x[0].rearrange("(i p) c -> p i c", p=128)),
                ("wc", wc[:, :, :], wcat.rearrange("(c p) n -> p c n", p=128)),
                ("wt", wt[:, :, :], wtT.rearrange("(c p) n -> p c n", p=128)),
                ("wtb", BW[:, :, ER], wtb.rearrange("(c p) -> p c", p=128)),
                ("wq", wq[:, :, :], wqT.rearrange("(c p) n -> p c n", p=128)),
                ("bq", bq_s[:, :], bq.rearrange("(c p) -> p c", p=128)),
                ("bkv", bkv_s[:, :], bkv.partition_broadcast(128)),
                ("bo", bo_s[:, :], bo.partition_broadcast(128)),
                ("scale", sc_s[:, :], scale.partition_broadcast(128)),
                ("As", As_s[:, :], As),
                ("wdb", W2[ER + 1:ER + 2, :], wdb.rearrange("(a n) -> a n", a=1)),
                ("wo", wo[:, :, :], woT.rearrange("(c p) n -> p c n", p=128)),
            ):
                q.inc(q.e.dma_start(dst, src, allow_slow_non_contiguous=name in ("wtb", "bq")),
                      S(name if name != "x0" else "x_0"), 16)
            q.wait(S("am0"), 1)
            q.inc(q.e.dma_start(Am_s[1:NL, 0:ER], Am[1:NL, :]), S("am"), 16)
        at("sp", -200, setup_loads)

        def setup_pool(q):
            q.inc(q.e.memset(idf[:, :], 0.0), S("id"))
            q.inc(q.e.memset(idb[:, :], 0.0), S("id"))
            q.wait(S("id"), 2)
            for m in (idf, idb):
                q.inc(q.e.affine_select(out=m[:, :], in_=m[:, :], compare_op=ALU.not_equal, fill=1.0,
                                        base=0, pattern=[[-1, 128]], channel_multiplier=1), S("id"))
        at("pool", -200, setup_pool)

        def setup_dve(q):
            q.inc(q.e.memset(Am_s[:, :], 1.0), S("amd"))
            q.wait(S("amd"), 1)
            q.inc(q.e.memset(Am_s[0:1, :], 0.0), S("am0"))
            q.inc(q.e.memset(K6[96:128, :, :], 1.0), S("ones"))
            q.inc(q.e.memset(VK[:, :, :, 32:48], 1.0), S("ones"))
            q.inc(q.e.memset(mkT[96:128, :], 1.0), S("ones"))
            q.inc(q.e.memset(MmT[96:128, :], 1.0), S("ones"))
            for e in range(NE):
                q.inc(q.e.memset(prio[:, e:e + 1], float(NE - e)), S("prio"))
        at("dve", -200, setup_dve)

        at("act", -300, lambda q: q.e.preload_act_table_set("natural_log_exp_and_others"))

        def scale_wq(q):
            q.wait(S("wq"), 16)
            q.wait(S("bq"), 16)
            q.inc(q.e.mul(wq[:, :, :], wq[:, :, :], D ** -0.5), S("wqs"))
            q.inc(q.e.mul(bq_s[:, :], bq_s[:, :], D ** -0.5), S("wqs"))
        at("act", -100, scale_wq)

        for name, src, dst, ready in (("wc", wc, wcr, ("wc", 16)), ("wq", wq, wqr, ("wqs", 2)),
                                      ("wo", wo, wor, ("wo", 16))):
            def whi(q, name=name, src=src, dst=dst, ready=ready):
                q.wait(S(ready[0]), ready[1])
                q.inc(q.e.copy(dst[:, 0, :, :], src[:, :, :]), S(name + "h"))
            at("act", -99, whi)

            def wlo(q, name=name, src=src, dst=dst):
                q.wait(S(name + "h"), 1)
                q.inc(q.e.tensor_tensor(dst[:, 1, :, :], src[:, :, :], dst[:, 0, :, :].bitcast(F32), ALU.subtract),
                      S(name + "l"))
            at("pool", -98, wlo)

        PARTS = ((0, 0), (1, 0), (0, 1))

        for h in range(2):
            def bw(q, bank, part, h=h):
                q.wait(S("wc"), 16)
                q.wait(S("wt"), 16)
                for c in range(2):
                    mm = q.e.matmul(bank[:, 0:ER], wt[:, c, 128 * h:128 * h + 128], wc[:, c, U0:WC],
                                    start=(c == 0), stop=(c == 1))
                q.inc(mm, S("bw"))
            job = misc(-150 + h, bw, (S("bwe"), h + 1), -148)

            def bwe(q, h=h, job=job):
                q.wait(S("bw"), h + 1)
                q.inc(q.e.copy(BW[:, h, 0:ER], job["bank"][:, 0:ER]), S("bwe"))
            at("act", -149 + h, bwe)

        def w2(q, bank, part):
            q.wait(S("bwe"), 2)
            q.wait(S("wtb"), 16)
            for c in range(2):
                mm = q.e.matmul(bank[0:ER + 1, 0:C], BW[:, c, :], wc[:, c, 0:C], start=(c == 0), stop=(c == 1))
            q.inc(mm, S("w2"))
        job_w2 = misc(-147, w2, (S("w2e"), 1), -146)

        def w2e(q):
            q.wait(S("w2"), 1)
            q.inc(q.e.copy(W2[0:ER + 1, :], job_w2["bank"][0:ER + 1, 0:C]), S("w2e"))
        at("act", -146, w2e)

        def before(b):
            t0 = 64 * (b - 1)
            xb, r = b % 2, b % 4
            n = b + 1

            def load(q):
                q.wait(S("xn"), 4 * (n - 2))
                q.wait(S("r0"), n - 2)
                q.inc(q.e.dma_start(X[:, xb, :, :], x[b].rearrange("(i p) c -> p i c", p=128)), S(f"x_{xb}"), 16)
            if b:
                at("sp", t0 - 67, load)

            def stats(q, i):
                q.wait(S(f"x_{xb}"), 16 * (b // 2 + 1))
                q.wait(S("mvd"), n - 1)
                q.inc(q.e.bn_stats(st[:, i, :], X[:, xb, i, :]), S("st"))
            for i in range(4):
                at("dve", t0 + (-60.2, -58.2, -54.2, -50.2)[i], lambda q, i=i: stats(q, i))

            def aggr(q):
                q.wait(S("st"), 4 * n)
                q.wait(S("xn"), 4 * (n - 1))
                for i in range(4):
                    ins = q.e.bn_aggr(mv[:, i, :], st[:, i, :])
                q.inc(ins, S("mvd"))
            at("dve", t0 - 45.2, aggr)

            def var(q):
                q.wait(S("mvd"), n)
                q.wait(S("ry"), n - 1)
                q.inc(q.e.tensor_scalar(ve[:, :], mv[:, :, 1], LN_EPS, None, ALU.add), S("ve"))
            at("dve", t0 - 43.2, var)

            def root(q):
                q.wait(S("ve"), n)
                q.wait(S("ry"), n - 1)
                q.inc(q.e.activation(lv[:, :], ve[:, :], ACT.Ln), S("lv"))
                q.wait(S("lv"), n)
                q.inc(q.e.activation(y0[:, :], lv[:, :], ACT.Exp, scale=-0.5), S("y0"))
            at("act", t0 - 41, root)

            def refine0(q):
                q.wait(S("y0"), n)
                q.inc(q.e.tensor_tensor(y2[:, :], y0[:, :], y0[:, :], ALU.mult), S("y2"))

            def refine1(q):
                q.wait(S("y2"), n)
                q.inc(q.e.tensor_tensor(y3[:, :], y2[:, :], ve[:, :], ALU.mult), S("y3"))

            def refine2(q):
                q.wait(S("y3"), n)
                q.inc(q.e.tensor_scalar(y4[:, :], y3[:, :], -0.5, 1.5, ALU.mult, ALU.add), S("y4"))

            def refine3(q):
                q.wait(S("y4"), n)
                q.inc(q.e.tensor_tensor(rstd[:, :], y4[:, :], y0[:, :], ALU.mult), S("ry"))
            chain("pool", t0 - 38, 0.1, (refine0, refine1, refine2, refine3))

            def norm(q, i):
                q.wait(S("ry"), n)
                q.wait(S("xt"), 2 * (n - 2))
                q.wait(S("r0"), n - 2)
                q.inc(q.e.tensor_scalar(XN[:, xb, i, :], X[:, xb, i, :], mv[:, i, 0:1], rstd[:, i:i + 1],
                                        ALU.subtract, ALU.mult), S("xn"))
            for i in range(4):
                at("dve", t0 - 10.2 + 2 * i, lambda q, i=i: norm(q, i))

            def residual(q):
                q.wait(S("xn"), 4 * n)
                q.wait(S("fo"), 2 * (n - 4))
                q.inc(q.e.tensor_tensor(Rs[:, r, :, :], X[:, xb, :, :], XN[:, xb, :, :], ALU.add), S("r0"))
                q.wait(S("r0"), n)
                q.wait(S("bo"), 16)
                q.inc(q.e.tensor_tensor(Rs[:, r, :, :], Rs[:, r, :, :],
                                        bo_s[:, :].unsqueeze(1).to_broadcast([128, 4, C]), ALU.add), S("r1"))
            at("pool", t0 + 3, residual)

            for c in range(2):
                def xt(q, bank, part, c=c):
                    q.wait(S("xn"), 4 * n)
                    q.wait(S("id"), 4)
                    for i in range(4):
                        mm = q.e.transpose(bank[:, 128 * i:128 * i + 128], XN[:, xb, i, 128 * c:128 * c + 128],
                                           idf[:, :])
                    q.inc(mm, S("xt"))
                job = misc(t0 + S_XT[c], xt, (S("xtl"), 2 * b + c + 1), t0 + S_XT[c] + 3)

                def xte(q, c=c, job=job):
                    q.wait(S("xt"), 2 * b + c + 1)
                    q.wait(S("j"), 4 * b)
                    q.wait(S("q"), 2 * b)
                    q.inc(q.e.copy(xT[:, 0, c, :], job["bank"][:, :]), S("xte"))
                at("act", t0 + S_XT[c] + 1.5, xte)

                def xtl(q, c=c, job=job):
                    q.wait(S("xte"), 2 * b + c + 1)
                    q.inc(q.e.tensor_tensor(xT[:, 1, c, :], job["bank"][:, :], xT[:, 0, c, :].bitcast(F32),
                                            ALU.subtract), S("xtl"))
                at("dve", t0 + S_XT[c] + 2.9, xtl)

            for i in range(4):
                def j(q, bank, part, i=i):
                    q.wait(S("xtl"), 2 * b + 2)
                    q.wait(S("wcl"), 1)
                    for k, (m, w) in enumerate(PARTS):
                        mm = q.e.matmul(bank[:, 0:WC], xT[:, m, part, 128 * i:128 * i + 128], wcr[:, w, part, :],
                                        start=(part == 0 and k == 0), stop=(part == 1 and k == 2))
                    if part == 1:
                        q.inc(mm, S("j"))
                job = misc(tuple(t0 + s for s in S_J[i]), j, (S("je"), 4 * b + i + 1), t0 + S_J[i][1] + 2)

                def je(q, i=i, job=job):
                    q.wait(S("j"), 4 * b + i + 1)
                    if i == 0:
                        q.wait(S("z"), 2 * b)
                        q.wait(S("ul"), b)
                    q.inc(q.e.copy(Jt[:, i, :], job["bank"][:, 0:WC]), S("je"))
                at("act", t0 + S_J[i][1] + 2, je)

            for g in range(2):
                tq = t0 + S_Q[g][1]

                def qt(q, bank, part, g=g):
                    q.wait(S("xtl"), 2 * b + 2)
                    q.wait(S("wql"), 1)
                    for k, (m, w) in enumerate(PARTS):
                        mm = q.e.matmul(bank[:, :], wqr[:, w, part, 128 * g:128 * g + 128], xT[:, m, part, :],
                                        start=(part == 0 and k == 0), stop=(part == 1 and k == 2))
                    if part == 1:
                        q.inc(mm, S("q"))
                job = misc(tuple(t0 + s for s in S_Q[g]), qt, (S("q1"), 2 * b + g + 1), tq + 3.4)

                def qh(q, g=g, job=job):
                    q.wait(S("q"), 2 * b + g + 1)
                    if b:
                        q.wait(S("qw"), 32 * b)
                    q.wait(S("wqs"), 2)
                    q.inc(q.e.activation(Qp[:, g, 0, :], job["bank"][:, :], ACT.Identity, bias=bq_s[:, g:g + 1]),
                          S("qh"))
                at("act", tq + 2, qh)

                def qr(q, g=g, job=job):
                    q.wait(S("qh"), 2 * b + g + 1)
                    q.wait(S("ql"), 2 * (b - 1) + g + 1)
                    q.inc(q.e.scalar_tensor_tensor(out=q1[:, g, :], in0=job["bank"][:, :], scalar=bq_s[:, g:g + 1],
                                                   in1=Qp[:, g, 0, :], op0=ALU.add, op1=ALU.subtract), S("q1"))
                at("dve", tq + 3.4, qr)

                def qm(q, g=g):
                    q.wait(S("q1"), 2 * b + g + 1)
                    q.inc(q.e.tensor_copy(Qp[:, g, 1, :], q1[:, g, :]), S("qm"))
                at("dve", tq + 4.4, qm)

                def ql(q, g=g):
                    q.wait(S("qm"), 2 * b + g + 1)
                    q.inc(q.e.tensor_tensor(Qp[:, g, 2, :], q1[:, g, :], Qp[:, g, 1, :], ALU.subtract), S("ql"))
                at("pool", tq + 5.6, ql)

                def qw(q, g=g):
                    q.wait(S("ql"), 2 * b + g + 1)
                    if b >= 2:
                        q.wait(S(f"qr_{xb}"), 96 * (b // 2))
                    q.inc(q.e.dma_start(qd[xb, :, 8 * g:8 * g + 8].rearrange("p h d t -> (h d) p t"),
                                        Qp[:, g, :, :]), S("qw"), 16)
                at("sp", tq + 8, qw)

            def qread(q):
                q.wait(S("qw"), 32 * n)
                if b >= 2:
                    q.wait(S("b"), 64 * (b - 1))
                for k, piece in enumerate((0, 0, 0, 1, 1, 2)):
                    q.inc(q.e.dma_start(Q6[16 * k:16 * k + 16, xb, :, :], qd[xb, piece].rearrange("h d t -> d h t")),
                          S(f"qr_{xb}"), 16)
            at("sp", t0 + 51, qread)

            v3 = b % 3

            def kv(q):
                q.wait(S("je"), 4 * n)
                q.wait(S("bkv"), 16)
                if b >= 3:
                    q.wait(S("pv"), 16 * (b - 2))
                q.inc(q.e.tensor_tensor(VK[:, v3, :, 0:32], Jt[:, :, KV0:G0],
                                        bkv_s[:, :].unsqueeze(1).to_broadcast([128, 4, 2 * D]), ALU.add), S("kv"))
            at("dve", t0 + 30, kv)

            kf = VK[:, v3, :, 0:16]
            sl = [K6t[:, :, 16 * k:16 * k + 16] for k in range(6)]

            def ks0(q):
                q.wait(S("kv"), n)
                q.wait(S("k6t"), n - 1)
                q.inc(q.e.tensor_copy(sl[0], kf), S("k0"))

            def ks1(q):
                q.wait(S("k0"), n)
                q.inc(q.e.tensor_tensor(k1[:, :, :], kf, sl[0], ALU.subtract), S("k1"))
                q.e.tensor_copy(sl[3], sl[0])
                q.e.tensor_copy(sl[5], sl[0])

            def ks2(q):
                q.wait(S("k1"), n)
                q.inc(q.e.tensor_copy(sl[1], k1[:, :, :]), S("k2"))

            def ks3(q):
                q.wait(S("k2"), n)
                q.inc(q.e.tensor_tensor(sl[2], k1[:, :, :], sl[1], ALU.subtract), S("k3"))
                q.inc(q.e.tensor_copy(sl[4], sl[1]), S("k6"))
            chain("pool", t0 + 32, 0.1, (ks0, ks1, ks2, ks3))

            def kt(q, bank, part):
                q.wait(S("k6"), n)
                q.wait(S("id"), 4)
                o = bank[:, :].bitcast(BF16)
                for i in range(4):
                    mm = q.e.transpose(o[0:96, 128 * i:128 * i + 128], K6t[:, i, :], idb[:, :])
                q.inc(mm, S("k6t"))
            job_k = misc(t0 + S_K, kt, (S("k6e"), n), t0 + S_K + 2)

            def kte(q):
                q.wait(S("k6t"), n)
                q.wait(S("ones"), 4)
                if b >= 3:
                    q.wait(S("b"), 64 * (b - 2))
                q.inc(q.e.copy(K6[0:96, v3, :], job_k["bank"][0:96, :].bitcast(BF16)[:, 0:T]), S("k6e"))
            at("act", t0 + S_K + 2, kte)

            gt = Jt[:, :, G0:U0]

            def gate0(q):
                q.wait(S("je"), 4 * n)
                q.inc(q.e.tensor_reduce(gmx[:, :], gt, AX, ALU.max), S("g0"))

            def gate1(q):
                q.wait(S("g0"), n)
                q.inc(q.e.tensor_tensor(geq[:, :, :], gt, bc(gmx[:, :], NE), ALU.is_equal), S("g1"))

            def gate2(q):
                q.wait(S("g1"), n)
                q.wait(S("prio"), NE)
                q.inc(q.e.tensor_tensor(gw[:, :, :], geq[:, :, :],
                                        prio[:, :].unsqueeze(1).to_broadcast([128, 4, NE]), ALU.mult), S("g2"))

            def gate3(q):
                q.wait(S("g2"), n)
                q.inc(q.e.tensor_reduce(gm2[:, :], gw[:, :, :], AX, ALU.max), S("g3"))

            def gate4(q):
                q.wait(S("g3"), n)
                q.wait(S("mk"), n - 1)
                q.inc(q.e.tensor_tensor(oh[:, :, :], gw[:, :, :], bc(gm2[:, :], NE), ALU.is_equal), S("oh"))
            chain("dve", t0 + 30.9, 1, (gate0, gate1, gate2, gate3, gate4))

            def mask(q):
                q.wait(S("oh"), n)
                q.wait(S("ut"), n - 1)
                q.wait(S("mkt"), n - 1)
                o4 = bc(oh[:, :, :], NR)
                q.inc(q.e.tensor_tensor(Um[:, :, :].rearrange("p i (e r) -> p i e r", r=NR),
                                        Jt[:, :, U0:WC].rearrange("p i (e r) -> p i e r", r=NR), o4, ALU.mult),
                      S("ul"))
                q.inc(q.e.tensor_copy(mk[:, :, :].rearrange("p i (e r) -> p i e r", r=NR), o4), S("mk"))
            at("pool", t0 + 36, mask)

            def ut(q, bank, part):
                q.wait(S("ul"), n)
                for i in range(4):
                    mm = q.e.transpose(bank[0:ER, 128 * i:128 * i + 128], Um[:, i, :], idf[:, :])
                q.inc(mm, S("ut"))
            job_u = misc(t0 + S_U, ut, (S("ute"), n), t0 + S_U + 2)

            def ute(q):
                q.wait(S("ut"), n)
                q.wait(S("sc"), n - 1)
                q.inc(q.e.copy(UT[0:ER, :], job_u["bank"][0:ER, :]), S("ute"))
            at("act", t0 + S_U + 2, ute)

            def mt(q, bank, part):
                q.wait(S("mk"), n)
                o = bank[:, :].bitcast(BF16)
                for i in range(4):
                    mm = q.e.transpose(o[0:ER, 128 * i:128 * i + 128], mk[:, i, :], idb[:, :])
                q.inc(mm, S("mkt"))
            job_m = misc(t0 + S_MK, mt, (S("mke"), n), t0 + S_MK + 2)

            def mke(q):
                q.wait(S("mkt"), n)
                q.wait(S("mm"), n - 1)
                q.inc(q.e.copy(mkT[0:ER, :], job_m["bank"][0:ER, :].bitcast(BF16)[:, 0:T]), S("mke"))
            at("act", t0 + S_MK + 2, mke)

            def sc(q, bank, part):
                q.wait(S("ute"), n)
                q.wait(S("As"), 16)
                for i in range(4):
                    mm = q.e.matmul(bank[:, NL * i:NL * i + NL], UT[0:ER, 128 * i:128 * i + 128], As_s[:, :],
                                    start=True, stop=True)
                q.inc(mm, S("sc"))
            job_s = misc(t0 + S_SC, sc, (S("sd"), n), t0 + S_SC + 4.2)

            def smax(q):
                v = job_s["bank"][:, 0:4 * NL].rearrange("p (i l) -> p i l", l=NL)
                q.wait(S("sc"), n)
                q.inc(q.e.tensor_reduce(smx[:, :], v, AX, ALU.max), S("sm"))

            def ssub(q):
                v = job_s["bank"][:, 0:4 * NL].rearrange("p (i l) -> p i l", l=NL)
                q.wait(S("sm"), n)
                q.wait(S("es"), n - 1)
                q.inc(q.e.tensor_tensor(Sd[:, :, :], v, bc(smx[:, :], NL), ALU.subtract), S("sd"))
            chain("dve", t0 + S_SC + 2.8, 1.2, (smax, ssub))

            def sexp(q):
                q.wait(S("sd"), n)
                q.wait(S("en"), n - 1)
                q.inc(q.e.activation(Es[:, :, :], Sd[:, :, :], ACT.Exp, scale=C ** -0.5), S("es"))
            at("act", t0 + S_SC + 5, sexp)

            def ssum(q):
                q.wait(S("es"), n)
                q.inc(q.e.tensor_reduce(sL[:, :], Es[:, :, :], AX, ALU.add), S("sl"))

            def srec(q):
                q.wait(S("sl"), n)
                q.wait(S("en"), n - 1)
                q.inc(q.e.reciprocal(sR[:, :], sL[:, :]), S("sr"))
            chain("dve", t0 + S_SC + 6.6, .9, (ssum, srec))

            def snorm(q):
                q.wait(S("sr"), n)
                q.wait(S("pt"), n - 1)
                q.inc(q.e.tensor_tensor(En[:, :, :], Es[:, :, :], bc(sR[:, :], NL), ALU.mult), S("en"))
            at("pool", t0 + S_SC + 8, snorm)

            def pt(q, bank, part):
                q.wait(S("en"), n)
                for i in range(4):
                    mm = q.e.transpose(bank[0:NL, 128 * i:128 * i + 128], En[:, i, :], idf[:, :])
                q.inc(mm, S("pt"))
            job_p = misc(t0 + S_PT, pt, (S("pte"), n), t0 + S_PT + 2)

            def pte(q):
                q.wait(S("pt"), n)
                q.wait(S("ma"), n - 1)
                q.inc(q.e.copy(PT[0:NL, :], job_p["bank"][0:NL, :]), S("pte"))
            at("act", t0 + S_PT + 2, pte)

            def ma(q, bank, part):
                q.wait(S("pte"), n)
                q.wait(S("am"), 16)
                q.inc(q.e.matmul(bank[0:ER + 1, :], Am_s[0:NL, :], PT[0:NL, :], start=True, stop=True), S("ma"))
            job_a = misc(t0 + S_MA, ma, (S("mm"), n), t0 + S_MA + 2.2)

            def mm_(q):
                q.wait(S("ma"), n)
                q.wait(S("mke"), n)
                q.wait(S("ones"), 4)
                q.wait(S("d"), 2 * (n - 1))
                q.inc(q.e.tensor_tensor(MmT[0:ER + 1, :], job_a["bank"][0:ER + 1, :], mkT[0:ER + 1, :], ALU.mult),
                      S("mm"))
            at("dve", t0 + S_MA + 2.2, mm_)

            for k in range(2):
                td = t0 + S_D[k][1]

                def dd(q, bank, part, k=k):
                    q.wait(S("mm"), n)
                    q.wait(S("w2e"), 1)
                    q.wait(S("wdb"), 16)
                    t = 2 * k + part
                    mm = q.e.matmul(bank[:, C * part:C * part + C], MmT[0:ER + 2, 128 * t:128 * t + 128],
                                    W2[0:ER + 2, :], start=True, stop=True)
                    if part == 1:
                        q.inc(mm, S("d"))
                job = misc(tuple(t0 + s for s in S_D[k]), dd, (S("z"), 2 * b + k + 1), td + 1.6)

                def zz(q, k=k, job=job):
                    q.wait(S("d"), 2 * b + k + 1)
                    q.wait(S("cx"), 2 * (n - 1))
                    q.wait(S("je"), 4 * n)
                    q.inc(q.e.tensor_tensor(Z[:, 2 * k:2 * k + 2, :],
                                            job["bank"][:, :].rearrange("p (i c) -> p i c", i=2),
                                            Jt[:, 2 * k:2 * k + 2, 0:C], ALU.add), S("z"))
                at("dve", td + 1.6, zz)

            def dexp(q, k):
                q.wait(S("z"), 2 * b + k + 1)
                q.wait(S("scale"), 16)
                q.wait(S("lg"), 2 * (n - 1))
                q.inc(q.e.activation(Cx[:, 2 * k:2 * k + 2, :], Z[:, 2 * k:2 * k + 2, :], ACT.Exp,
                                     scale=sc_s[:, 0:1]), S("cx"))
            at("act", t0 + 78, lambda q: dexp(q, 0))
            at("act", t0 + 80, lambda q: dexp(q, 1))

            def guard(q):
                q.wait(S("cx"), 2 * n)
                q.inc(q.e.tensor_scalar(Cz[:, :, :], Cx[:, :, :], 0.0, F32_EPS, ALU.is_equal, ALU.mult), S("c0"))
                q.wait(S("c0"), n)
                q.inc(q.e.tensor_tensor(Cx[:, :, :], Cx[:, :, :], Cz[:, :, :], ALU.add), S("c1"))
            at("pool", t0 + 81.5, guard)

            def dlog(q, k):
                q.wait(S("c1"), n)
                q.wait(S("r2"), n - 1)
                q.inc(q.e.activation(Cz[:, 2 * k:2 * k + 2, :], Cx[:, 2 * k:2 * k + 2, :], ACT.Ln), S("lg"))
            at("act", t0 + 93, lambda q: dlog(q, 0))
            at("act", t0 + 94, lambda q: dlog(q, 1))

            def radd(q):
                q.wait(S("lg"), 2 * n)
                q.wait(S("r1"), n)
                q.inc(q.e.tensor_tensor(Rs[:, r, :, :], Rs[:, r, :, :], Cz[:, :, :], ALU.add), S("r2"))
            at("pool", t0 + 105, radd)

        for b in range(NB):
            before(b)

        for n in range(64 * NB):
            b, qq, h = n // 64, n % 64 // 16, n % 16
            g = n // 16

            def a(q, n=n, b=b, qq=qq, h=h):
                if n % 64 == 0:
                    q.wait(S(f"qr_{b % 2}"), 96 * (b // 2 + 1))
                    q.wait(S("k6e"), b + 1)
                q.wait(S("mx"), n - 1)
                q.inc(q.e.matmul(pA[n % 2][:, :], Q6[0:96, b % 2, h, 128 * qq:128 * qq + 128],
                                 K6[0:96, b % 3, :], start=True, stop=True), S("a"))
            at("pe", n, a)

            def mx(q, n=n, g=g, h=h):
                q.wait(S("a"), n + 1)
                q.wait(S("m0"), 2 * (g - 1))
                q.inc(q.e.tensor_reduce(M[:, g % 2, h:h + 1], pA[n % 2][:, :], AX, ALU.max, negate=True), S("mx"))
            at("dve", n + 0.5, mx)

        for g in range(4 * NB):
            b, qq = g // 4, g % 4
            t1 = 16 * g + 16
            mg = M[:, g % 2, :]

            def ms(q, g=g, mg=mg):
                m1 = M1[:, g % 2, :]
                q.wait(S("mx"), 16 * g + 16)
                q.wait(S("mt"), g)
                q.inc(q.e.tensor_copy(M3[:, 0, :], mg), S("mh"))
                q.wait(S("mh"), g + 1)
                q.inc(q.e.tensor_tensor(m1, mg, M3[:, 0, :], ALU.subtract), S("m0"))

            def ms2(q, g=g):
                m1 = M1[:, g % 2, :]
                q.wait(S("m0"), 2 * g + 1)
                q.inc(q.e.tensor_copy(M3[:, 1, :], m1), S("mm1"))
                q.wait(S("mm1"), g + 1)
                q.inc(q.e.tensor_tensor(M3[:, 2, :], m1, M3[:, 1, :], ALU.subtract), S("m0"))
            chain("dve", t1 - 0.3, 1, (ms, ms2))

            def mtp(q, bank, part, g=g):
                q.wait(S("m0"), 2 * g + 2)
                q.wait(S("id"), 4)
                q.inc(q.e.transpose(bank[:, :].bitcast(BF16)[0:48, 0:128],
                                    M3[:, :, :].rearrange("p k h -> p (k h)"), idb[:, :]), S("mt"))
            job = misc(t1 + 3, mtp, (S("mte"), g + 1), t1 + 5)

            def mte(q, g=g, job=job):
                q.wait(S("mt"), g + 1)
                if g >= 2:
                    q.wait(S(f"md_{g % 2}"), 48 * (g // 2))
                q.inc(q.e.copy(MT[:, g % 2, :], job["bank"][0:48, :].bitcast(BF16)[:, 0:128]), S("mte"))
            at("act", t1 + 5, mte)

            def md(q, g=g, b=b, qq=qq):
                q.wait(S("mte"), g + 1)
                if b >= 2:
                    q.wait(S("b"), 64 * (b - 1))
                for k in range(3):
                    q.inc(q.e.dma_start(Q6[96 + k:97 + k, b % 2, :, 128 * qq:128 * qq + 128],
                                        MT[16 * k:16 * k + 16, g % 2, :]), S(f"md_{g % 2}"), 16)
            at("sp", t1 + 6, md)

        for u in range(64 * NB):
            b, g, i, j = u // 64, u % 64 // 16, u % 16 // 4, u % 4
            gg = u // 16

            def bs(q, u=u, b=b, i=i, j=j, g=g, gg=gg):
                if u % 16 == 0:
                    q.wait(S(f"md_{gg % 2}"), 48 * (gg // 2 + 1))
                q.wait(S("e"), u - 1)
                hh = 4 * g + j
                q.inc(q.e.matmul(pB[u % 2][:, :], K6[0:99, b % 3, 128 * i:128 * i + 128],
                                 Q6[0:99, b % 2, :, 32 * hh:32 * hh + 32], start=True, stop=True), S("b"))
            at("pe", u + LB + 0.3, bs)

            def ex(q, u=u):
                q.wait(S("b"), u + 1)
                if u >= PR:
                    q.wait(S("pv"), (u - PR) // 4 + 1)
                q.inc(q.e.activation(P[:, u % PR, :], pB[u % 2][:, :], ACT.Exp), S("e"))
            at("act", u + LB + 0.6, ex)

        for w in range(16 * NB):
            b, g, i = w // 16, w % 16 // 4, w % 4
            gg = w // 4

            def pv(q, w=w, b=b, i=i, gg=gg):
                q.wait(S("e"), 4 * w + 4)
                q.wait(S("kv"), b + 1)
                q.wait(S("ones"), 4)
                if i == 0:
                    q.wait(S("ot"), gg - 1)
                for j in range(4):
                    mm = q.e.matmul(pO[gg % 2][32 * j:32 * j + 32, :], VK[:, b % 3, i, 16:48],
                                    P[:, (4 * w + j) % PR, :], start=(i == 0), stop=(i == 3))
                q.inc(mm, S("pv"))
            at("pe", 4 * w + LB + LP, pv)

        for gg in range(4 * NB):
            b, g = gg // 4, gg % 4
            t2 = 16 * gg + LB + LP + 12
            hf = g // 2
            nh = 2 * b + hf

            def ot(q, gg=gg):
                q.wait(S("pv"), 4 * gg + 4)
                if gg >= 2:
                    q.wait(S(f"ow_{gg % 2}"), 64 * (gg // 2))
                q.inc(q.e.copy(OTr[:, gg % 2, :], pO[gg % 2][:, :]), S("ot"))
            at("act", t2 + 2, ot)

            def ow(q, gg=gg, b=b, g=g, hf=hf):
                q.wait(S("ot"), gg + 1)
                if b >= 2:
                    q.wait(S("or"), 32 * (2 * (b - 2) + hf + 1))
                for j in range(4):
                    q.inc(q.e.dma_start(od[b % 2, hf, :, 4 * (g % 2) + j, :], OTr[32 * j:32 * j + 32, gg % 2, :]),
                          S(f"ow_{gg % 2}"), 16)
            at("sp", t2 + 3.3, ow)

            if g % 2 == 0:
                continue

            def orr(q, nh=nh, b=b, hf=hf, gg=gg):
                q.wait(S("ow_0"), 64 * (nh + 1))
                q.wait(S("ow_1"), 64 * (nh + 1))
                q.wait(S("ov"), nh)
                v = od[b % 2, hf].rearrange("r h t -> (r h) t")
                q.inc(q.e.dma_start(Lb[:, :], v[128:256, :]), S("or"), 16)
                q.inc(q.e.dma_start(Op[:, :], v[0:128, :]), S("or"), 16)
            at("sp", t2 + 7, orr)

            def lr(q, nh=nh):
                q.wait(S("or"), 32 * (nh + 1))
                q.wait(S("ov"), nh)
                q.inc(q.e.activation(Ln1[:, :], Lb[:, :], ACT.Ln), S("l0"))

            def lr2(q, nh=nh):
                q.wait(S("l0"), nh + 1)
                q.wait(S("ov"), nh)
                q.inc(q.e.activation(Ly[:, :], Ln1[:, :], ACT.Exp, scale=-1.0), S("l1"))
            chain("act", t2 + 11, 1, (lr, lr2))

            def on(q, nh=nh, b=b, hf=hf):
                q.wait(S("l1"), nh + 1)
                q.inc(q.e.tensor_tensor(Ln1[:, :], Lb[:, :], Ly[:, :], ALU.mult), S("n0"))
                q.wait(S("n0"), nh + 1)
                q.inc(q.e.tensor_scalar(Ln1[:, :], Ln1[:, :], -1.0, 2.0, ALU.mult, ALU.add), S("n1"))
                q.wait(S("n1"), nh + 1)
                q.inc(q.e.tensor_tensor(Ln1[:, :], Ln1[:, :], Ly[:, :], ALU.mult), S("o0"))
                q.wait(S("o0"), nh + 1)
                q.wait(S("on"), nh)
                q.inc(q.e.tensor_tensor(Ov[:, :].rearrange("p (t h) -> p h t", h=H),
                                        Op[:, :].rearrange("p (h t) -> p h t", h=H),
                                        Ln1[:, :].rearrange("p (h t) -> p h t", h=H), ALU.mult), S("ov"))
            at("pool", t2 + 14, on)

            def onh(q, nh=nh, b=b, hf=hf):
                q.wait(S("ov"), nh + 1)
                q.wait(S("fo"), 2 * b)
                q.inc(q.e.copy(On[:, 0, hf, :], Ov[:, :]), S("onh"))
            at("act", t2 + 21, onh)

            def onl(q, nh=nh, hf=hf):
                q.wait(S("onh"), nh + 1)
                q.inc(q.e.tensor_tensor(On[:, 1, hf, :], Ov[:, :], On[:, 0, hf, :].bitcast(F32), ALU.subtract),
                      S("on"))
            at("pool", t2 + 22, onl)

        for b in range(NB):
            for k in range(2):
                t3 = 64 * b + S_O[k][1]

                def oo(q, bank, part, b=b, k=k):
                    q.wait(S("on"), 2 * b + 2)
                    q.wait(S("wol"), 1)
                    t = 2 * k + part
                    for c in range(2):
                        for k, (m, w) in enumerate(PARTS):
                            mm = q.e.matmul(bank[:, C * part:C * part + C], On[:, m, c, 128 * t:128 * t + 128],
                                            wor[:, w, c, :], start=(c == 0 and k == 0), stop=(c == 1 and k == 2))
                    if part == 1:
                        q.inc(mm, S("o"))
                job = misc(tuple(64 * b + s for s in S_O[k]), oo, (S("fo"), 2 * b + k + 1), t3 + 2)

                def fo(q, b=b, k=k, job=job):
                    m = 2 * b + k
                    q.wait(S("o"), m + 1)
                    q.wait(S("r2"), b + 1)
                    if m >= 2:
                        q.wait(S(f"st_{k}"), 16 * b)
                    q.inc(q.e.tensor_tensor(OUT[:, k, :, :], job["bank"][:, :].rearrange("p (i c) -> p i c", i=2),
                                            Rs[:, b % 4, 2 * k:2 * k + 2, :], ALU.add), S("fo"))
                at("dve", t3 + 2, fo)

                def store(q, b=b, k=k):
                    q.wait(S("fo"), 2 * b + k + 1)
                    q.inc(q.e.dma_start(out[b, 256 * k:256 * k + 256, :].rearrange("(i p) c -> p i c", p=128),
                                        OUT[:, k, :, :]), S(f"st_{k}"), 16)
                at("sp", t3 + 4, store)

        def finish(q):
            for k in range(2):
                q.wait(S(f"st_{k}"), 16 * NB)
            for k in range(2):
                q.wait(S(f"qr_{k}"), 96 * (NB // 2))
                q.wait(S(f"ow_{k}"), 64 * 2 * NB)
        at("sp", 1e9, finish)

        jobs.sort(key=lambda j: j["slots"])
        for n, job in enumerate(jobs):
            job["bank"] = pM[n % 2]
            if n >= 2:
                assert jobs[n - 2]["rslot"] <= job["slots"][0], (n, jobs[n - 2]["slots"], job["slots"])
            if n >= 1:
                assert jobs[n - 1]["slots"][-1] < job["slots"][0], (n, jobs[n - 1]["slots"], job["slots"])
            for part, slot in enumerate(job["slots"]):
                def run(q, n=n, job=job, part=part):
                    if n >= 2 and part == 0:
                        q.wait(*jobs[n - 2]["release"])
                    job["fn"](q, job["bank"], part)
                at("pe", slot + 0.15, run)

        block = ctx.enter_context(nc.Block())

        @block.tensor
        def _(e):
            plan.emit("pe", e)

        @block.scalar
        def _(e):
            plan.emit("act", e)

        @block.vector
        def _(e):
            plan.emit("dve", e)

        @block.gpsimd
        def _(e):
            plan.emit("pool", e)

        @block.sync
        def _(e):
            plan.emit("sp", e)

    return plan


def kernel(**inputs):
    import numpy as np
    import concourse.bacc as bacc
    from concourse.bass_utils import run_bass_kernel_spmd

    a = {k: np.asarray(v) for k, v in inputs.items()}
    AA, BB = a["L0_ffn_A"], a["L0_ffn_B"]
    arrays = {
        "x": a["L0_attn_x"],
        "wcat": np.concatenate([a["L0_ffn_wd_w"].T, a["L0_attn_Wkv"].T, a["L0_ffn_w_gate"],
                                BB.reshape(ER, C).T], axis=1),
        "wqT": a["L0_attn_Wq"].T,
        "woT": a["L0_attn_Wo"].T.reshape(2, 8, D, C).transpose(0, 2, 1, 3).reshape(C, C),
        "wtT": a["L0_ffn_wt_w"].T,
        "wtb": a["L0_ffn_wt_b"],
        "bq": a["L0_attn_bq"],
        "bkv": a["L0_attn_bkv"],
        "bo": a["L0_attn_bo"],
        "wdb": a["L0_ffn_wd_b"],
        "As": AA.transpose(0, 2, 1).reshape(ER, NL),
        "Am": AA.transpose(1, 0, 2).reshape(NL, ER),
        "scale": a["L0_ffn_scale"],
    }
    nc = bacc.Bacc("TRN2", target_bir_lowering=False, num_devices=1)
    args, feed = [], {}
    for name, v in arrays.items():
        v = np.ascontiguousarray(v)
        feed[f"in_{name}"] = v
        args.append(nc.dram_tensor(f"in_{name}", v.shape, mybir.dt.from_np(v.dtype), kind="ExternalInput").ap())
    o = nc.dram_tensor("out_0", (NB, T, C), F32, kind="ExternalOutput").ap()
    build(nc, *args, o)
    r = run_bass_kernel_spmd(nc, [feed], core_ids=[0])
    return r.results[0]["out_0"]
```

```python
from contextlib import ExitStack

import concourse.bass as bass
from concourse import mybir

F32 = mybir.dt.float32
BF16 = mybir.dt.bfloat16
F32R = mybir.dt.float32r
ALU = mybir.AluOpType
ACT = mybir.ActivationFunctionType
AX = mybir.AxisListType.X

NB = 16
T = 512
C = 256
H = 16
D = 16
NE = 6
NL = 100
NR = 16
ER = NE * NR
WC = C + 2 * D + NE + ER
KV0, G0, U0 = C, C + 2 * D, C + 2 * D + NE
LN_EPS = 1e-5
F32_EPS = 1.1920928955078125e-07
NA = 3
LA = 0
PR = 12
LB = 26
LP = 11

BEFORE = {
    "load": -67, "stats0": -41.44, "stats1": -40.67, "stats2": -44.82, "stats3": -49.86, "aggr": -38.58,
    "var": -33.0, "root": -33.36, "refine": -26.31, "norm0": -11.47, "norm1": -6.71, "norm2": 0.35,
    "norm3": 3.74, "residual": 5.27, "xt0": 6.29, "xt1": 10, "xte0": 9.21, "xte1": 11.5, "xtl0": 9.9,
    "xtl1": 11.46, "j0": 13.17, "j1": 16, "j2": 23, "j3": 23.48, "j0+": 14.34, "j1+": 18.76, "j2+": 24,
    "j3+": 25.48, "je0": 15.42, "je1": 20, "je2": 24, "je3": 26, "q0": 28, "q1": 36, "q0+": 30.85,
    "q1+": 39.02, "qh0": 31.53, "qh1": 40, "qr0": 32.68, "qr1": 41.4, "qm0": 35.2, "qm1": 43.2, "ql0": 35.3,
    "ql1": 43.3, "qw0": 37.18, "qw1": 46.56, "qread": 49.52, "kv": 27, "ks": 27.37, "k": 34.07, "u": 39.38,
    "m": 42, "s": 43, "p": 55.02, "a": 58.03, "kte": 34, "ute": 41.32, "mke": 42.04, "gate0": 26.75,
    "gate1": 28.49, "gate2": 29.03, "gate3": 30.27, "gate4": 31.15, "mask": 32.9, "smax": 44.01,
    "ssub": 45.8, "sexp": 48, "ssum": 50.69, "srec": 52.26, "snorm": 50.07, "pte": 56, "mm": 59.9,
    "d0": 66.67, "d1": 75, "d0+": 67.19, "d1+": 75.5, "zz0": 68.48, "zz1": 75.19, "dexp0": 78.7,
    "dexp1": 80, "guard": 81.5, "dlog0": 92.84, "dlog1": 93.47, "radd": 105, "mmh": 60.77, "mml": 62.7,
}
FIRST = {
    "bqs": 11.7, "wqs": 7.15, "wqh": 8.5, "wql": 9, "wch": 1.63, "wcl": 9.6, "woh": 9.64, "wol": 18.98,
    "residual": 42, "bw0": 24.78, "bw1": 26, "bwe0": 26.48, "bwe1": 27.3, "w2": 28.5, "w2e": 29.5, "u": 33,
    "ute": 34, "m": 33.5, "mke": 35, "s": 36, "smax": 63.91, "ssub": 64.4, "sexp": 66.08, "ssum": 65.64,
    "srec": 71.44, "snorm": 68, "p": 75, "pte": 76, "a": 80, "mm": 79.62, "d0": 83.88, "d0+": 84.38,
    "zz0": 84.02, "d1": 85.52, "d1+": 86.02, "zz1": 86.4, "dexp0": 88, "dexp1": 100.06, "guard": 101.37,
    "dlog0": 107, "dlog1": 108, "radd": 112, "k": 27.1, "kte": 27.6, "kv": 26.02, "ks": 26.55, "q0": 12,
    "q0+": 14, "qh0": 14.5, "qr0": 15, "qm0": 15.1, "ql0": 16.1, "qw0": 16, "q1": 14.67, "q1+": 15.17,
    "qh1": 16.5, "qr1": 17, "qm1": 17.1, "ql1": 17.2, "qw1": 18, "qread": 20, "j0": 17.93, "j0+": 18.93,
    "je0": 21, "j1": 20, "j1+": 21, "je1": 22.45, "j2": 22, "j2+": 23, "je2": 25, "j3": 24, "j3+": 24.02,
    "je3": 26.41, "norm3": 9.39, "mmh": 82.4, "mml": 82.8, "w2h": 29.83, "w2l": 39.2, "stats1": -41.02,
    "gate1": 28.31,
}
SECOND = {
    "load": -66.24, "mask": 30.48, "ssub": 46.07, "m": 40.29, "stats0": -44.47, "xtl0": 9.39, "xte0": 7.49,
    "q0": 27.68, "q0+": 32.05, "xt0": 6.47, "sexp": 49.94, "qh1": 41.28, "a": 58.96, "k": 33.47,
    "j0": 13.17, "j0+": 14.63, "je2": 23.5, "qr0": 32.67, "zz1": 77.04, "j1": 16, "j1+": 16.5, "mml": 61.23,
    "mke": 41.33, "u": 40.18, "d0": 66.47, "d0+": 66.99, "qread": 59.47, "root": -32.08, "gate4": 31.89,
    "pte": 56.11,
}
AFTER = {
    "ms0": 0.01, "ms1": 0.7, "mt": 3.19, "mte": 5, "md": 9.15, "ot": 2.03, "ow": 2.82, "or": 9.44, "on": 14,
    "onh": 22.31, "onl": 25.89, "lr0": 10.59, "lr1": 11.26, "o0": 123, "o0+": 124, "fo0": 126,
    "st0": 130.59, "o1": 126, "o1+": 127, "fo1": 129, "st1": 131.31,
}
LAST = {
    "mt": 1, "mte": 1.2, "md": 2, "or": 9.44, "lr0": 15.88, "lr1": 23.24, "on": 18, "onh": 27.31, "onl": 29,
}


class Plan:

    def __init__(self):
        self.items = {e: [] for e in ("pe", "act", "dve", "pool", "sp")}
        self.seq = 0

    def at(self, engine, slot, fn):
        self.seq += 1
        self.items[engine].append((slot, self.seq, fn))

    def emit(self, engine, e):
        done = {}
        for _, _, fn in sorted(self.items[engine], key=lambda t: t[:2]):
            fn(Queue(e, done))


class Queue:

    def __init__(self, e, done):
        self.e, self.done = e, done

    def wait(self, sem, value):
        if value > self.done.get(id(sem), 0):
            self.done[id(sem)] = value
            self.e.wait_ge(sem, value)

    def inc(self, ins, sem, n=1):
        ins.then_inc(sem, n)


def build(nc, x, wcat, wqT, woT, wtT, wtb, bq, bkv, bo, wdb, As, Am, scale, out):
    plan = Plan()
    at = plan.at
    ctx = ExitStack()
    with ctx:
        def sb(name, shape, dt=F32):
            return ctx.enter_context(nc.sbuf_tensor(name, shape, dt))

        def ps(name):
            return ctx.enter_context(nc.psum_tensor(name, [128, 512], F32))

        sems = {}

        def S(name):
            if name not in sems:
                sems[name] = ctx.enter_context(nc.semaphore("s_" + name))
            return sems[name]

        X = sb("X", [128, 2, 4, C])
        XN = sb("XN", [128, 2, 4, C])
        Rs = sb("Rs", [128, 4, 4, C])
        st = sb("st", [128, 4, 6])
        mv = sb("mv", [128, 4, 2])
        ve = sb("ve", [128, 4])
        lv = sb("lv", [128, 4])
        y0 = sb("y0", [128, 4])
        y2 = sb("y2", [128, 4])
        y3 = sb("y3", [128, 4])
        y4 = sb("y4", [128, 4])
        rstd = sb("rstd", [128, 4])
        xT = sb("xT", [128, 2, 2, T], F32R)
        wcr = sb("wcr", [128, 2, 2, WC], F32R)
        wqr = sb("wqr", [128, 2, 2, C], F32R)
        wor = sb("wor", [128, 2, 2, C], F32R)
        Jt = sb("Jt", [128, 2, 4, WC])
        Qp = sb("Qp", [128, 2, 3, T], BF16)
        q1 = sb("q1", [128, 2, T])
        Q6 = sb("Q6", [128, 2, H, T], BF16)
        VK = sb("VK", [128, 3, 4, 48])
        K6t = sb("K6t", [128, 4, 96], BF16)
        k1 = sb("k1", [128, 4, 16])
        K6 = sb("K6", [128, 3, T], BF16)
        Um = sb("Um", [128, 4, ER])
        mk = sb("mk", [128, 4, ER], BF16)
        UT = sb("UT", [128, T])
        mkT = sb("mkT", [128, T], BF16)
        gmx = sb("gmx", [128, 4])
        geq = sb("geq", [128, 4, NE])
        gw = sb("gw", [128, 4, NE])
        gm2 = sb("gm2", [128, 4])
        oh = sb("oh", [128, 4, NE])
        smx = sb("smx", [128, 4])
        Sd = sb("Sd", [128, 4, NL])
        Es = sb("Es", [128, 4, NL])
        sL = sb("sL", [128, 4])
        sR = sb("sR", [128, 4])
        En = sb("En", [128, 4, NL])
        PT = sb("PT", [128, T])
        MmT = sb("MmT", [128, T])
        MmR = sb("MmR", [128, 2, T], F32R)
        W2r = sb("W2r", [128, 2, C], F32R)
        Cx = sb("Cx", [128, 4, C])
        Cz = sb("Cz", [128, 4, C])
        P = sb("P", [128, PR, T])
        M = sb("M", [128, 2, H])
        M1 = sb("M1", [128, 2, H])
        M3 = sb("M3", [128, 3, H], BF16)
        MT = sb("MT", [48, 2, 128], BF16)
        OTr = sb("OTr", [128, 2, T])
        Op = sb("Op", [128, T])
        Lb = sb("Lb", [128, T])
        Ln1 = sb("Ln1", [128, T])
        Ly = sb("Ly", [128, T])
        Ov = sb("Ov", [128, T])
        On = sb("On", [128, 2, 2, T], F32R)
        OUT = sb("OUT", [128, 2, 2, C])
        wc = sb("wc", [128, 2, WC])
        wq = sb("wq", [128, 2, C])
        wo = sb("wo", [128, 2, C])
        wt = sb("wt", [128, 2, C])
        BW = sb("BW", [128, 2, ER + 1])
        W2 = sb("W2", [128, C])
        As_s = sb("As_s", [ER, NL])
        Am_s = sb("Am_s", [128, ER + 1])
        bq_s = sb("bq_s", [128, 2])
        bkv_s = sb("bkv_s", [128, 2 * D])
        bo_s = sb("bo_s", [128, C])
        sc_s = sb("sc_s", [128, 1])
        idf = sb("idf", [128, 128])
        idb = sb("idb", [128, 128], BF16)
        prio = sb("prio", [128, NE])

        pA = [ps(f"pA{k}") for k in range(NA)]
        pB = [ps("pB0"), ps("pB1")]
        pO = ps("pO")
        pM = [ps("pM0"), ps("pM1")]

        qd = nc.dram_tensor("q_pieces", (2, 3, H, D, T), BF16, kind="Internal").ap()
        od = nc.dram_tensor("o_parts", (2, 2, 8, 2, D, T), F32, kind="Internal").ap()

        def bc(ap, n):
            return ap.unsqueeze(len(ap.shape)).to_broadcast(list(ap.shape) + [n])

        jobs = []

        def misc(slots, fn, release):
            slots = slots if isinstance(slots, tuple) else (slots,)
            job = {"slots": slots, "fn": fn, "release": release}
            jobs.append(job)
            return job

        def chain(engine, slot, step, steps):
            for n, fn in enumerate(steps):
                at(engine, slot + step * n, fn)

        def setup_loads(q):
            for name, dst, src in (
                ("x0", X[:, 0, :, :], x[0].rearrange("(i p) c -> p i c", p=128)),
                ("wq", wq[:, :, :], wqT.rearrange("(c p) n -> p c n", p=128)),
                ("wc", wc[:, :, :], wcat.rearrange("(c p) n -> p c n", p=128)),
                ("bq", bq_s[:, :], bq.rearrange("(c p) -> p c", p=128)),
                ("bkv", bkv_s[:, :], bkv.partition_broadcast(128)),
                ("wt", wt[:, :, :], wtT.rearrange("(c p) n -> p c n", p=128)),
                ("wtb", BW[:, :, ER], wtb.rearrange("(c p) -> p c", p=128)),
                ("bo", bo_s[:, :], bo.partition_broadcast(128)),
                ("scale", sc_s[:, :], scale.partition_broadcast(128)),
                ("As", As_s[:, :], As),
                ("wdb", W2[ER + 1:ER + 2, :], wdb.rearrange("(a n) -> a n", a=1)),
                ("wo", wo[:, :, :], woT.rearrange("(c p) n -> p c n", p=128)),
            ):
                q.inc(q.e.dma_start(dst, src, allow_slow_non_contiguous=name in ("wtb", "bq")),
                      S(name if name != "x0" else "x_0"), 16)
            q.wait(S("am0"), 1)
            q.inc(q.e.dma_start(Am_s[1:NL, 0:ER], Am[1:NL, :]), S("am"), 16)
        at("sp", -200, setup_loads)

        def setup_pool(q):
            q.inc(q.e.memset(idf[:, :], 0.0), S("id"))
            q.inc(q.e.memset(idb[:, :], 0.0), S("id"))
            q.wait(S("id"), 2)
            for m in (idf, idb):
                q.inc(q.e.affine_select(out=m[:, :], in_=m[:, :], compare_op=ALU.not_equal, fill=1.0,
                                        base=0, pattern=[[-1, 128]], channel_multiplier=1), S("id"))
        at("pool", -200, setup_pool)

        def setup_dve(q):
            q.inc(q.e.memset(Am_s[:, :], 1.0), S("amd"))
            q.wait(S("amd"), 1)
            q.inc(q.e.memset(Am_s[0:1, :], 0.0), S("am0"))
            q.inc(q.e.memset(K6[96:128, :, :], 1.0), S("ones"))
            q.inc(q.e.memset(VK[:, :, :, 32:48], 1.0), S("ones"))
            q.inc(q.e.memset(mkT[96:128, :], 1.0), S("ones"))
            q.inc(q.e.memset(MmT[96:128, :], 1.0), S("ones"))
            for e in range(NE):
                q.inc(q.e.memset(prio[:, e:e + 1], float(NE - e)), S("prio"))
        at("dve", -200, setup_dve)

        at("act", -300, lambda q: q.e.preload_act_table_set("natural_log_exp_and_others"))

        def scale_bq(q):
            q.wait(S("bq"), 16)
            q.inc(q.e.mul(bq_s[:, :], bq_s[:, :], D ** -0.5), S("bqs"))
        at("act", FIRST["bqs"] - 64, scale_bq)

        def scale_wq(q):
            q.wait(S("wq"), 16)
            q.inc(q.e.tensor_scalar(wq[:, :, :], wq[:, :, :], D ** -0.5, None, ALU.mult), S("wqs"))
        at("dve", FIRST["wqs"] - 64, scale_wq)

        for name, src, dst, ready in (("wq", wq, wqr, ("wqs", 1)), ("wc", wc, wcr, ("wc", 16)),
                                      ("wo", wo, wor, ("wo", 16))):
            def whi(q, name=name, src=src, dst=dst, ready=ready):
                q.wait(S(ready[0]), ready[1])
                q.inc(q.e.copy(dst[:, 0, :, :], src[:, :, :]), S(name + "h"))
            at("act", FIRST[name + "h"] - 64, whi)

            def wlo(q, name=name, src=src, dst=dst):
                q.wait(S(name + "h"), 1)
                q.inc(q.e.tensor_tensor(dst[:, 1, :, :], src[:, :, :], dst[:, 0, :, :].bitcast(F32), ALU.subtract),
                      S(name + "l"))
            at("pool", FIRST[name + "l"] - 64, wlo)

        PARTS = ((0, 0), (1, 0), (0, 1))

        for h in range(2):
            def bw(q, bank, part, h=h):
                q.wait(S("wc"), 16)
                q.wait(S("wt"), 16)
                for c in range(2):
                    mm = q.e.matmul(bank[:, 0:ER], wt[:, c, 128 * h:128 * h + 128], wc[:, c, U0:WC],
                                    start=(c == 0), stop=(c == 1))
                q.inc(mm, S("bw"))
            job = misc(FIRST[f"bw{h}"] - 64, bw, (S("bwe"), h + 1))

            def bwe(q, h=h, job=job):
                q.wait(S("bw"), h + 1)
                q.inc(q.e.copy(BW[:, h, 0:ER], job["bank"][:, 0:ER]), S("bwe"))
            at("act", FIRST[f"bwe{h}"] - 64, bwe)

        def w2(q, bank, part):
            q.wait(S("bwe"), 2)
            q.wait(S("wtb"), 16)
            for c in range(2):
                mm = q.e.matmul(bank[0:ER + 1, 0:C], BW[:, c, :], wc[:, c, 0:C], start=(c == 0), stop=(c == 1))
            q.inc(mm, S("w2"))
        job_w2 = misc(FIRST["w2"] - 64, w2, (S("w2e"), 1))

        def w2e(q):
            q.wait(S("w2"), 1)
            q.inc(q.e.copy(W2[0:ER + 1, :], job_w2["bank"][0:ER + 1, 0:C]), S("w2e"))
        at("act", FIRST["w2e"] - 64, w2e)

        def w2h(q):
            q.wait(S("w2e"), 1)
            q.wait(S("wdb"), 16)
            q.inc(q.e.copy(W2r[0:ER + 2, 0, :], W2[0:ER + 2, :]), S("w2h"))
        at("act", FIRST["w2h"] - 64, w2h)

        def w2l(q):
            q.wait(S("w2h"), 1)
            q.inc(q.e.tensor_tensor(W2r[0:ER + 2, 1, :], W2[0:ER + 2, :], W2r[0:ER + 2, 0, :].bitcast(F32),
                                    ALU.subtract), S("w2l"))
        at("pool", FIRST["w2l"] - 64, w2l)

        def before(b):
            t0 = 64 * (b - 1)
            xb, r = b % 2, b % 4
            n = b + 1

            def L(name):
                return t0 + ((FIRST, SECOND)[b].get(name, BEFORE[name]) if b < 2 else BEFORE[name])

            def load(q):
                q.wait(S("xn"), 4 * (n - 2))
                q.wait(S("r0"), n - 2)
                q.inc(q.e.dma_start(X[:, xb, :, :], x[b].rearrange("(i p) c -> p i c", p=128)), S(f"x_{xb}"), 16)
            if b:
                at("sp", L("load"), load)

            def stats(q, i):
                q.wait(S(f"x_{xb}"), 16 * (b // 2 + 1))
                q.wait(S("mvd"), n - 1)
                q.inc(q.e.bn_stats(st[:, i, :], X[:, xb, i, :]), S("st"))
            for i in range(4):
                at("dve", L(f"stats{i}"), lambda q, i=i: stats(q, i))

            def aggr(q):
                q.wait(S("st"), 4 * n)
                q.wait(S("xn"), 4 * (n - 1))
                for i in range(4):
                    ins = q.e.bn_aggr(mv[:, i, :], st[:, i, :])
                q.inc(ins, S("mvd"))
            at("dve", L("aggr"), aggr)

            def var(q):
                q.wait(S("mvd"), n)
                q.wait(S("ry"), n - 1)
                q.inc(q.e.tensor_scalar(ve[:, :], mv[:, :, 1], LN_EPS, None, ALU.add), S("ve"))
            at("dve", L("var"), var)

            def root(q):
                q.wait(S("ve"), n)
                q.wait(S("ry"), n - 1)
                q.inc(q.e.activation(lv[:, :], ve[:, :], ACT.Ln), S("lv"))
                q.wait(S("lv"), n)
                q.inc(q.e.activation(y0[:, :], lv[:, :], ACT.Exp, scale=-0.5), S("y0"))
            at("act", L("root"), root)

            def refine0(q):
                q.wait(S("y0"), n)
                q.inc(q.e.tensor_tensor(y2[:, :], y0[:, :], y0[:, :], ALU.mult), S("y2"))

            def refine1(q):
                q.wait(S("y2"), n)
                q.inc(q.e.tensor_tensor(y3[:, :], y2[:, :], ve[:, :], ALU.mult), S("y3"))

            def refine2(q):
                q.wait(S("y3"), n)
                q.inc(q.e.tensor_scalar(y4[:, :], y3[:, :], -0.5, 1.5, ALU.mult, ALU.add), S("y4"))

            def refine3(q):
                q.wait(S("y4"), n)
                q.inc(q.e.tensor_tensor(rstd[:, :], y4[:, :], y0[:, :], ALU.mult), S("ry"))
            chain("dve" if b == 0 else "pool", L("refine"), 0.1, (refine0, refine1, refine2, refine3))

            def norm(q, i):
                q.wait(S("ry"), n)
                q.wait(S("xt"), 2 * (n - 2))
                q.wait(S("r0"), n - 2)
                q.inc(q.e.tensor_scalar(XN[:, xb, i, :], X[:, xb, i, :], mv[:, i, 0:1], rstd[:, i:i + 1],
                                        ALU.subtract, ALU.mult), S("xn"))
            for i in range(4):
                at("dve", L(f"norm{i}"), lambda q, i=i: norm(q, i))

            def residual(q):
                q.wait(S("xn"), 4 * n)
                q.wait(S("fo"), 2 * (n - 4))
                q.inc(q.e.tensor_tensor(Rs[:, r, :, :], X[:, xb, :, :], XN[:, xb, :, :], ALU.add), S("r0"))
                q.wait(S("r0"), n)
                q.wait(S("bo"), 16)
                q.inc(q.e.tensor_tensor(Rs[:, r, :, :], Rs[:, r, :, :],
                                        bo_s[:, :].unsqueeze(1).to_broadcast([128, 4, C]), ALU.add), S("r1"))
            at("pool", L("residual"), residual)

            for c in range(2):
                def xt(q, bank, part, c=c):
                    q.wait(S("id"), 4)
                    for i in range(4):
                        q.wait(S("xn"), 4 * b + i + 1 if b == 0 else 4 * n)
                        mm = q.e.transpose(bank[:, 128 * i:128 * i + 128], XN[:, xb, i, 128 * c:128 * c + 128],
                                           idf[:, :])
                    q.inc(mm, S("xt"))
                job = misc(L(f"xt{c}"), xt, (S("xtl"), 2 * b + c + 1))

                def xte(q, c=c, job=job):
                    q.wait(S("xt"), 2 * b + c + 1)
                    q.wait(S("j"), 4 * b)
                    q.wait(S("q"), 2 * b)
                    q.inc(q.e.copy(xT[:, 0, c, :], job["bank"][:, :]), S("xte"))
                at("act", L(f"xte{c}"), xte)

                def xtl(q, c=c, job=job):
                    q.wait(S("xte"), 2 * b + c + 1)
                    q.inc(q.e.tensor_tensor(xT[:, 1, c, :], job["bank"][:, :], xT[:, 0, c, :].bitcast(F32),
                                            ALU.subtract), S("xtl"))
                at("dve", L(f"xtl{c}"), xtl)

            for i in range(4):
                def j(q, bank, part, i=i):
                    q.wait(S("xtl"), 2 * b + 1 + part)
                    q.wait(S("wcl"), 1)
                    for k, (m, w) in enumerate(PARTS):
                        mm = q.e.matmul(bank[:, 0:WC], xT[:, m, part, 128 * i:128 * i + 128], wcr[:, w, part, :],
                                        start=(part == 0 and k == 0), stop=(part == 1 and k == 2))
                    if part == 1:
                        q.inc(mm, S("j"))
                job = misc((L(f"j{i}"), L(f"j{i}+")), j, (S("je"), 4 * b + i + 1))

                def je(q, i=i, job=job):
                    q.wait(S("j"), 4 * b + i + 1)
                    if i == 0:
                        q.wait(S("z"), 2 * (b - 1))
                        q.wait(S("ul"), b - 1)
                        q.wait(S("oh"), b - 1)
                        q.wait(S("kv"), b - 1)
                    q.inc(q.e.copy(Jt[:, xb, i, :], job["bank"][:, 0:WC]), S("je"))
                at("act", L(f"je{i}"), je)

            for g in range(2):
                def qt(q, bank, part, g=g):
                    q.wait(S("xtl"), 2 * b + 1 + part)
                    q.wait(S("wql"), 1)
                    for k, (m, w) in enumerate(PARTS):
                        mm = q.e.matmul(bank[:, :], wqr[:, w, part, 128 * g:128 * g + 128], xT[:, m, part, :],
                                        start=(part == 0 and k == 0), stop=(part == 1 and k == 2))
                    if part == 1:
                        q.inc(mm, S("q"))
                job = misc((L(f"q{g}"), L(f"q{g}+")), qt, (S("q1"), 2 * b + g + 1))

                def qh(q, g=g, job=job):
                    q.wait(S("q"), 2 * b + g + 1)
                    if b:
                        q.wait(S("qw"), 32 * b)
                    q.wait(S("bqs"), 1)
                    q.inc(q.e.activation(Qp[:, g, 0, :], job["bank"][:, :], ACT.Identity, bias=bq_s[:, g:g + 1]),
                          S("qh"))
                at("act", L(f"qh{g}"), qh)

                def qr(q, g=g, job=job):
                    q.wait(S("qh"), 2 * b + g + 1)
                    q.wait(S("ql"), 2 * (b - 1) + g + 1)
                    q.inc(q.e.scalar_tensor_tensor(out=q1[:, g, :], in0=job["bank"][:, :], scalar=bq_s[:, g:g + 1],
                                                   in1=Qp[:, g, 0, :], op0=ALU.add, op1=ALU.subtract), S("q1"))
                at("dve", L(f"qr{g}"), qr)

                def qm(q, g=g):
                    q.wait(S("q1"), 2 * b + g + 1)
                    q.inc(q.e.tensor_copy(Qp[:, g, 1, :], q1[:, g, :]), S("qm"))
                at("dve" if b == 0 else "pool", L(f"qm{g}"), qm)

                def ql(q, g=g):
                    q.wait(S("qm"), 2 * b + g + 1)
                    q.inc(q.e.tensor_tensor(Qp[:, g, 2, :], q1[:, g, :], Qp[:, g, 1, :], ALU.subtract), S("ql"))
                at("dve" if b == 0 else "pool", L(f"ql{g}"), ql)

                def qw(q, g=g):
                    q.wait(S("ql"), 2 * b + g + 1)
                    if b >= 2:
                        q.wait(S(f"qr_{xb}"), 96 * (b // 2))
                    q.inc(q.e.dma_start(qd[xb, :, 8 * g:8 * g + 8].rearrange("p h d t -> (h d) p t"),
                                        Qp[:, g, :, :]), S("qw"), 16)
                at("sp", L(f"qw{g}"), qw)

            def qread(q):
                q.wait(S("qw"), 32 * n)
                if b >= 2:
                    q.wait(S("b"), 64 * (b - 1))
                for t, sem in (((0, 256), "qf"), ((256, T), "qr_0")) if b == 0 else (((0, T), f"qr_{xb}"),):
                    for k, piece in enumerate((0, 0, 0, 1, 1, 2)):
                        q.inc(q.e.dma_start(Q6[16 * k:16 * k + 16, xb, :, t[0]:t[1]],
                                            qd[xb, piece, :, :, t[0]:t[1]].rearrange("h d t -> d h t")), S(sem), 16)
            at("sp", L("qread"), qread)

            v3 = b % 3

            def kv(q):
                q.wait(S("je"), 4 * n)
                q.wait(S("bkv"), 16)
                if b >= 3:
                    q.wait(S("pv"), 16 * (b - 2))
                q.inc(q.e.tensor_tensor(VK[:, v3, :, 0:32], Jt[:, xb, :, KV0:G0],
                                        bkv_s[:, :].unsqueeze(1).to_broadcast([128, 4, 2 * D]), ALU.add), S("kv"))
            at("dve" if b == 0 else "pool", L("kv"), kv)

            kf = VK[:, v3, :, 0:16]
            sl = [K6t[:, :, 16 * k:16 * k + 16] for k in range(6)]

            def ks0(q):
                q.wait(S("kv"), n)
                q.wait(S("k6t"), n - 1)
                q.inc(q.e.tensor_copy(sl[0], kf), S("k0"))

            def ks1(q):
                q.wait(S("k0"), n)
                q.inc(q.e.tensor_tensor(k1[:, :, :], kf, sl[0], ALU.subtract), S("k1"))
                q.e.tensor_copy(sl[3], sl[0])
                q.e.tensor_copy(sl[5], sl[0])

            def ks2(q):
                q.wait(S("k1"), n)
                q.inc(q.e.tensor_copy(sl[1], k1[:, :, :]), S("k2"))

            def ks3(q):
                q.wait(S("k2"), n)
                q.inc(q.e.tensor_tensor(sl[2], k1[:, :, :], sl[1], ALU.subtract), S("k3"))
                q.inc(q.e.tensor_copy(sl[4], sl[1]), S("k6"))
            chain("dve" if b == 0 else "pool", L("ks"), 0.1, (ks0, ks1, ks2, ks3))

            def kt(q, bank, part):
                q.wait(S("k6"), n)
                q.wait(S("id"), 4)
                o = bank[:, :].bitcast(BF16)
                for i in range(4):
                    mm = q.e.transpose(o[0:96, 128 * i:128 * i + 128], K6t[:, i, :], idb[:, :])
                q.inc(mm, S("k6t"))
            job_k = misc(L("k"), kt, (S("k6e"), n))

            def kte(q):
                q.wait(S("k6t"), n)
                q.wait(S("ones"), 4)
                if b >= 3:
                    q.wait(S("b"), 64 * (b - 2))
                q.inc(q.e.copy(K6[0:96, v3, :], job_k["bank"][0:96, :].bitcast(BF16)[:, 0:T]), S("k6e"))
            at("act", L("kte"), kte)

            gt = Jt[:, xb, :, G0:U0]

            def gate0(q):
                q.wait(S("je"), 4 * n)
                q.inc(q.e.tensor_reduce(gmx[:, :], gt, AX, ALU.max), S("g0"))

            def gate1(q):
                q.wait(S("g0"), n)
                q.inc(q.e.tensor_tensor(geq[:, :, :], gt, bc(gmx[:, :], NE), ALU.is_equal), S("g1"))

            def gate2(q):
                q.wait(S("g1"), n)
                q.wait(S("prio"), NE)
                q.inc(q.e.tensor_tensor(gw[:, :, :], geq[:, :, :],
                                        prio[:, :].unsqueeze(1).to_broadcast([128, 4, NE]), ALU.mult), S("g2"))

            def gate3(q):
                q.wait(S("g2"), n)
                q.inc(q.e.tensor_reduce(gm2[:, :], gw[:, :, :], AX, ALU.max), S("g3"))

            def gate4(q):
                q.wait(S("g3"), n)
                q.wait(S("mk"), n - 1)
                q.inc(q.e.tensor_tensor(oh[:, :, :], gw[:, :, :], bc(gm2[:, :], NE), ALU.is_equal), S("oh"))
            for k, fn in enumerate((gate0, gate1, gate2, gate3, gate4)):
                at("dve", L(f"gate{k}"), fn)

            def mask(q):
                q.wait(S("oh"), n)
                q.wait(S("ut"), n - 1)
                q.wait(S("mkt"), n - 1)
                o4 = bc(oh[:, :, :], NR)
                q.inc(q.e.tensor_tensor(Um[:, :, :].rearrange("p i (e r) -> p i e r", r=NR),
                                        Jt[:, xb, :, U0:WC].rearrange("p i (e r) -> p i e r", r=NR), o4, ALU.mult),
                      S("ul"))
                q.inc(q.e.tensor_copy(mk[:, :, :].rearrange("p i (e r) -> p i e r", r=NR), o4), S("mk"))
            at("pool", L("mask"), mask)

            def ut(q, bank, part):
                q.wait(S("ul"), n)
                for i in range(4):
                    mm = q.e.transpose(bank[0:ER, 128 * i:128 * i + 128], Um[:, i, :], idf[:, :])
                q.inc(mm, S("ut"))
            job_u = misc(L("u"), ut, (S("ute"), n))

            def ute(q):
                q.wait(S("ut"), n)
                q.wait(S("sc"), n - 1)
                q.inc(q.e.copy(UT[0:ER, :], job_u["bank"][0:ER, :]), S("ute"))
            at("act", L("ute"), ute)

            def mt(q, bank, part):
                q.wait(S("mk"), n)
                o = bank[:, :].bitcast(BF16)
                for i in range(4):
                    mm = q.e.transpose(o[0:ER, 128 * i:128 * i + 128], mk[:, i, :], idb[:, :])
                q.inc(mm, S("mkt"))
            job_m = misc(L("m"), mt, (S("mke"), n))

            def mke(q):
                q.wait(S("mkt"), n)
                q.wait(S("mm"), n - 1)
                q.inc(q.e.copy(mkT[0:ER, :], job_m["bank"][0:ER, :].bitcast(BF16)[:, 0:T]), S("mke"))
            at("act", L("mke"), mke)

            def sc(q, bank, part):
                q.wait(S("ute"), n)
                q.wait(S("As"), 16)
                for i in range(4):
                    mm = q.e.matmul(bank[:, NL * i:NL * i + NL], UT[0:ER, 128 * i:128 * i + 128], As_s[:, :],
                                    start=True, stop=True)
                q.inc(mm, S("sc"))
            job_s = misc(L("s"), sc, (S("sd"), n))

            def smax(q):
                v = job_s["bank"][:, 0:4 * NL].rearrange("p (i l) -> p i l", l=NL)
                q.wait(S("sc"), n)
                q.inc(q.e.tensor_reduce(smx[:, :], v, AX, ALU.max), S("sm"))

            def ssub(q):
                v = job_s["bank"][:, 0:4 * NL].rearrange("p (i l) -> p i l", l=NL)
                q.wait(S("sm"), n)
                q.wait(S("es"), n - 1)
                q.inc(q.e.tensor_tensor(Sd[:, :, :], v, bc(smx[:, :], NL), ALU.subtract), S("sd"))
            at("dve", L("smax"), smax)
            at("dve", L("ssub"), ssub)

            def sexp(q):
                q.wait(S("sd"), n)
                q.wait(S("en"), n - 1)
                q.inc(q.e.activation(Es[:, :, :], Sd[:, :, :], ACT.Exp, scale=C ** -0.5), S("es"))
            at("act", L("sexp"), sexp)

            def ssum(q):
                q.wait(S("es"), n)
                q.inc(q.e.tensor_reduce(sL[:, :], Es[:, :, :], AX, ALU.add), S("sl"))

            def srec(q):
                q.wait(S("sl"), n)
                q.wait(S("en"), n - 1)
                q.inc(q.e.reciprocal(sR[:, :], sL[:, :]), S("sr"))
            at("dve", L("ssum"), ssum)
            at("dve", L("srec"), srec)

            def snorm(q):
                q.wait(S("sr"), n)
                q.wait(S("pt"), n - 1)
                q.inc(q.e.tensor_tensor(En[:, :, :], Es[:, :, :], bc(sR[:, :], NL), ALU.mult), S("en"))
            at("pool", L("snorm"), snorm)

            def pt(q, bank, part):
                q.wait(S("en"), n)
                for i in range(4):
                    mm = q.e.transpose(bank[0:NL, 128 * i:128 * i + 128], En[:, i, :], idf[:, :])
                q.inc(mm, S("pt"))
            job_p = misc(L("p"), pt, (S("pte"), n))

            def pte(q):
                q.wait(S("pt"), n)
                q.wait(S("ma"), n - 1)
                q.inc(q.e.copy(PT[0:NL, :], job_p["bank"][0:NL, :]), S("pte"))
            at("act", L("pte"), pte)

            def ma(q, bank, part):
                q.wait(S("pte"), n)
                q.wait(S("am"), 16)
                q.inc(q.e.matmul(bank[0:ER + 1, :], Am_s[0:NL, :], PT[0:NL, :], start=True, stop=True), S("ma"))
            job_a = misc(L("a"), ma, (S("mm"), n))

            def mm_(q):
                q.wait(S("ma"), n)
                q.wait(S("mke"), n)
                q.wait(S("ones"), 4)
                q.wait(S("mml"), n - 1)
                q.inc(q.e.tensor_tensor(MmT[0:ER + 1, :], job_a["bank"][0:ER + 1, :], mkT[0:ER + 1, :], ALU.mult),
                      S("mm"))
            at("dve", L("mm"), mm_)

            def mmh(q):
                q.wait(S("mm"), n)
                q.wait(S("d"), 2 * (n - 1))
                q.inc(q.e.copy(MmR[0:ER + 2, 0, :], MmT[0:ER + 2, :]), S("mmh"))
            at("act", L("mmh"), mmh)

            def mml(q):
                q.wait(S("mmh"), n)
                q.inc(q.e.tensor_tensor(MmR[0:ER + 2, 1, :], MmT[0:ER + 2, :], MmR[0:ER + 2, 0, :].bitcast(F32),
                                        ALU.subtract), S("mml"))
            at("pool", L("mml"), mml)

            for k in range(2):
                def dd(q, bank, part, k=k):
                    q.wait(S("mml"), n)
                    q.wait(S("w2l"), 1)
                    t = 2 * k + part
                    for k3, (m, w) in enumerate(PARTS):
                        mm = q.e.matmul(bank[:, C * part:C * part + C], MmR[0:ER + 2, m, 128 * t:128 * t + 128],
                                        W2r[0:ER + 2, w, :], start=(k3 == 0), stop=(k3 == 2))
                    if part == 1:
                        q.inc(mm, S("d"))
                job = misc((L(f"d{k}"), L(f"d{k}+")), dd, (S("z"), 2 * b + k + 1))

                def zz(q, k=k, job=job):
                    q.wait(S("d"), 2 * b + k + 1)
                    q.wait(S("lg"), 2 * (n - 1))
                    q.wait(S("je"), 4 * n)
                    q.inc(q.e.tensor_tensor(Cx[:, 2 * k:2 * k + 2, :],
                                            job["bank"][:, :].rearrange("p (i c) -> p i c", i=2),
                                            Jt[:, xb, 2 * k:2 * k + 2, 0:C], ALU.add), S("z"))
                at("dve", L(f"zz{k}"), zz)

            def dexp(q, k):
                q.wait(S("z"), 2 * b + k + 1)
                q.wait(S("scale"), 16)
                q.inc(q.e.activation(Cx[:, 2 * k:2 * k + 2, :], Cx[:, 2 * k:2 * k + 2, :], ACT.Exp,
                                     scale=sc_s[:, 0:1]), S("cx"))
            at("act", L("dexp0"), lambda q: dexp(q, 0))
            at("act", L("dexp1"), lambda q: dexp(q, 1))

            def guard(q):
                q.wait(S("cx"), 2 * n)
                q.inc(q.e.tensor_scalar(Cz[:, :, :], Cx[:, :, :], 0.0, F32_EPS, ALU.is_equal, ALU.mult), S("c0"))
                q.wait(S("c0"), n)
                q.inc(q.e.tensor_tensor(Cx[:, :, :], Cx[:, :, :], Cz[:, :, :], ALU.add), S("c1"))
            at("pool", L("guard"), guard)

            def dlog(q, k):
                q.wait(S("c1"), n)
                q.wait(S("r2"), n - 1)
                q.inc(q.e.activation(Cz[:, 2 * k:2 * k + 2, :], Cx[:, 2 * k:2 * k + 2, :], ACT.Ln), S("lg"))
            at("act", L("dlog0"), lambda q: dlog(q, 0))
            at("act", L("dlog1"), lambda q: dlog(q, 1))

            def radd(q):
                q.wait(S("lg"), 2 * n)
                q.wait(S("r1"), n)
                q.inc(q.e.tensor_tensor(Rs[:, r, :, :], Rs[:, r, :, :], Cz[:, :, :], ALU.add), S("r2"))
            at("pool", L("radd"), radd)

        for b in range(NB):
            before(b)

        for n in range(64 * NB):
            b, qq, h = n // 64, n % 64 // 16, n % 16
            g = n // 16

            def a(q, n=n, b=b, qq=qq, h=h):
                if n == 0:
                    q.wait(S("qf"), 96)
                if n == 32 or n and n % 64 == 0:
                    q.wait(S(f"qr_{b % 2}"), 96 * (b // 2 + 1))
                if n % 64 == 0:
                    q.wait(S("k6e"), b + 1)
                q.wait(S("mx"), n - NA + 1)
                q.inc(q.e.matmul(pA[n % NA][:, :], Q6[0:96, b % 2, h, 128 * qq:128 * qq + 128],
                                 K6[0:96, b % 3, :], start=True, stop=True), S("a"))
            at("pe", n - LA, a)

            def mx(q, n=n, g=g, h=h):
                q.wait(S("a"), n + 1)
                q.wait(S("m0"), 2 * (g - 1))
                q.inc(q.e.tensor_reduce(M[:, g % 2, h:h + 1], pA[n % NA][:, :], AX, ALU.max, negate=True), S("mx"))
            at("dve", n + 0.5, mx)

        for g in range(4 * NB):
            b, qq = g // 4, g % 4
            t1 = 16 * g + 16
            mg = M[:, g % 2, :]

            def ms(q, g=g, mg=mg):
                m1 = M1[:, g % 2, :]
                q.wait(S("mx"), 16 * g + 16)
                q.wait(S("mt"), g)
                q.inc(q.e.tensor_copy(M3[:, 0, :], mg), S("mh"))
                q.wait(S("mh"), g + 1)
                q.inc(q.e.tensor_tensor(m1, mg, M3[:, 0, :], ALU.subtract), S("m0"))

            def ms2(q, g=g):
                m1 = M1[:, g % 2, :]
                q.wait(S("m0"), 2 * g + 1)
                q.inc(q.e.tensor_copy(M3[:, 1, :], m1), S("mm1"))
                q.wait(S("mm1"), g + 1)
                q.inc(q.e.tensor_tensor(M3[:, 2, :], m1, M3[:, 1, :], ALU.subtract), S("m0"))
            at("dve", t1 + AFTER["ms0"], ms)
            at("dve", t1 + AFTER["ms1"], ms2)

            def mtp(q, bank, part, g=g):
                q.wait(S("m0"), 2 * g + 2)
                q.wait(S("id"), 4)
                q.inc(q.e.transpose(bank[:, :].bitcast(BF16)[0:48, 0:128],
                                    M3[:, :, :].rearrange("p k h -> p (k h)"), idb[:, :]), S("mt"))
            A = {**AFTER, **LAST} if g == 4 * NB - 1 else AFTER
            job = misc(t1 + A["mt"], mtp, (S("mte"), g + 1))

            def mte(q, g=g, job=job):
                q.wait(S("mt"), g + 1)
                if g >= 2:
                    q.wait(S(f"md_{g % 2}"), 16 * (g // 2))
                q.inc(q.e.copy(MT[:, g % 2, :], job["bank"][0:48, :].bitcast(BF16)[:, 0:128]), S("mte"))
            at("act", t1 + A["mte"], mte)

            def md(q, g=g, b=b, qq=qq):
                q.wait(S("mte"), g + 1)
                if b >= 2:
                    q.wait(S("b"), 64 * (b - 1))
                q.inc(q.e.dma_start(Q6[96:99, b % 2, :, 128 * qq:128 * qq + 128], MT[:, g % 2, :]),
                      S(f"md_{g % 2}"), 16)
            at("sp", t1 + A["md"], md)

        tail = 64 * NB - 16

        def score_bank(u):
            return pB[u % 2] if u < tail else (*pB, *pA)[(u - tail) % (2 + NA)]

        for u in range(64 * NB):
            b, g, i, j = u // 64, u % 64 // 16, u % 16 // 4, u % 4
            gg = u // 16

            def bs(q, u=u, b=b, i=i, j=j, g=g, gg=gg):
                if u % 16 == 0:
                    q.wait(S(f"md_{gg % 2}"), 16 * (gg // 2 + 1))
                if u < tail + 2:
                    q.wait(S("e"), u - 1)
                elif u < tail + 2 + NA:
                    q.wait(S("mx"), 64 * NB)
                else:
                    q.wait(S("e"), u - 1 - NA)
                hh = 4 * g + j
                q.inc(q.e.matmul(score_bank(u)[:, :], K6[0:99, b % 3, 128 * i:128 * i + 128],
                                 Q6[0:99, b % 2, :, 32 * hh:32 * hh + 32], start=True, stop=True), S("b"))
            at("pe", u + LB + 0.3, bs)

            def ex(q, u=u):
                q.wait(S("b"), u + 1)
                if u >= PR:
                    q.wait(S("pv"), (u - PR) // 4 + 1)
                q.inc(q.e.activation(P[:, u % PR, :], score_bank(u)[:, :], ACT.Exp), S("e"))
            at("act", u + LB + 0.6, ex)

        for w in range(16 * NB):
            b, g, i = w // 16, w % 16 // 4, w % 4
            gg = w // 4

            def pv(q, w=w, b=b, i=i, gg=gg):
                q.wait(S("e"), 4 * w + 4)
                q.wait(S("kv"), b + 1)
                q.wait(S("ones"), 4)
                if i == 0:
                    q.wait(S("ot"), gg)
                for j in range(4):
                    mm = q.e.matmul(pO[32 * j:32 * j + 32, :], VK[:, b % 3, i, 16:48],
                                    P[:, (4 * w + j) % PR, :], start=(i == 0), stop=(i == 3))
                q.inc(mm, S("pv"))
            at("pe", 4 * w + LB + LP, pv)

        OpX = X[:, NB % 2, 0:2, :].rearrange("p i c -> p (i c)")
        LbX = X[:, NB % 2, 2:4, :].rearrange("p i c -> p (i c)")
        for gg in range(4 * NB):
            b, g = gg // 4, gg % 4
            t2 = 16 * gg + LB + LP + 12
            hf = g // 2
            nh = 2 * b + hf
            last = nh == 2 * NB - 1

            A = {**AFTER, **LAST} if nh == 2 * NB - 2 else AFTER
            L_, O_ = (LbX, OpX) if last else (Lb, Op)
            spare = gg >= 4 * NB - 2

            def ot(q, gg=gg, spare=spare):
                q.wait(S("pv"), 4 * gg + 4)
                if gg >= 2:
                    q.wait(S(f"ow_{gg % 2}"), 16 * (gg // 2))
                copy = q.e.tensor_copy if spare else q.e.copy
                q.inc(copy(OTr[:, gg % 2, :], pO[:, :]), S("ot"))
            at("dve" if spare else "act", t2 + AFTER["ot"], ot)

            def ow(q, gg=gg, b=b, g=g, hf=hf):
                q.wait(S("ot"), gg + 1)
                if b >= 2:
                    q.wait(S("or"), 32 * (2 * (b - 2) + hf + 1))
                v = od[b % 2, hf, 4 * (g % 2):4 * (g % 2) + 4].rearrange("j s r t -> (j s r) t")
                q.inc(q.e.dma_start(v, OTr[:, gg % 2, :]), S(f"ow_{gg % 2}"), 16)

            def ow_last(q, gg=gg, nh=nh):
                q.wait(S("ot"), gg + 1)
                q.wait(S("xn"), 4 * (NB - 1))
                q.wait(S("r0"), NB - 1)
                for dst, row, sem in ((LbX, 16, "lb"), (OpX, 0, "op")):
                    for j in range(4):
                        p = 64 * (gg % 2) + 16 * j
                        q.inc(q.e.dma_start(dst[p:p + 16, :], OTr[32 * j + row:32 * j + row + 16, gg % 2, :]),
                              S(sem), 16)
            at("sp", t2 + AFTER["ow"], ow_last if last else ow)

            if g % 2 == 0:
                continue

            def orr(q, nh=nh, b=b, hf=hf, gg=gg):
                q.wait(S("ow_0"), 16 * (nh + 1))
                q.wait(S("ow_1"), 16 * (nh + 1))
                q.wait(S("ov"), nh)
                q.inc(q.e.dma_start(Lb[:, :], od[b % 2, hf, :, 1]), S("or"), 16)
                q.inc(q.e.dma_start(Op[:, :], od[b % 2, hf, :, 0]), S("or"), 16)
            if not last:
                at("sp", t2 + A["or"], orr)

            def lr(q, nh=nh, last=last, L_=L_):
                if last:
                    q.wait(S("lb"), 64 * 2)
                else:
                    q.wait(S("or"), 32 * (nh + 1))
                q.wait(S("ov"), nh)
                q.inc(q.e.activation(Ln1[:, :], L_[:, :], ACT.Ln), S("l0"))

            def lr2(q, nh=nh):
                q.wait(S("l0"), nh + 1)
                q.wait(S("ov"), nh)
                q.inc(q.e.activation(Ly[:, :], Ln1[:, :], ACT.Exp, scale=-1.0), S("l1"))
            at("act", t2 + A["lr0"], lr)
            at("act", t2 + A["lr1"], lr2)

            def on(q, nh=nh, last=last, L_=L_, O_=O_):
                q.wait(S("l1"), nh + 1)
                q.inc(q.e.tensor_tensor(Ln1[:, :], L_[:, :], Ly[:, :], ALU.mult), S("n0"))
                q.wait(S("n0"), nh + 1)
                q.inc(q.e.tensor_scalar(Ln1[:, :], Ln1[:, :], -1.0, 2.0, ALU.mult, ALU.add), S("n1"))
                q.wait(S("n1"), nh + 1)
                q.inc(q.e.tensor_tensor(Ln1[:, :], Ln1[:, :], Ly[:, :], ALU.mult), S("o0"))
                q.wait(S("o0"), nh + 1)
                if last:
                    q.wait(S("op"), 64 * 2)
                q.wait(S("on"), nh)
                q.inc(q.e.tensor_tensor(Ov[:, :].rearrange("p (t h) -> p h t", h=H),
                                        O_[:, :].rearrange("p (h t) -> p h t", h=H),
                                        Ln1[:, :].rearrange("p (h t) -> p h t", h=H), ALU.mult), S("ov"))
            at("dve" if last else "pool", t2 + A["on"], on)

            def onh(q, nh=nh, b=b, hf=hf):
                q.wait(S("ov"), nh + 1)
                q.wait(S("fo"), 2 * b)
                q.inc(q.e.copy(On[:, 0, hf, :], Ov[:, :]), S("onh"))
            at("act", t2 + A["onh"], onh)

            def onl(q, nh=nh, hf=hf):
                q.wait(S("onh"), nh + 1)
                q.inc(q.e.tensor_tensor(On[:, 1, hf, :], Ov[:, :], On[:, 0, hf, :].bitcast(F32), ALU.subtract),
                      S("on"))
            at("dve" if last else "pool", t2 + A["onl"], onl)

        for b in range(NB):
            for k in range(2):
                t3 = 64 * b

                def oo(q, bank, part, b=b, k=k):
                    q.wait(S("on"), 2 * b + 1 + part)
                    q.wait(S("wol"), 1)
                    for i in range(2):
                        t = 2 * k + i
                        for n, (m, w) in enumerate(PARTS):
                            mm = q.e.matmul(bank[:, C * i:C * i + C], On[:, m, part, 128 * t:128 * t + 128],
                                            wor[:, w, part, :], start=(part == 0 and i == 0 and n == 0),
                                            stop=(part == 1 and i == 1 and n == 2))
                    if part == 1:
                        q.inc(mm, S("o"))
                slots = (t3 + AFTER[f"o{k}"] if b < NB - 1 else 64 * b + 110 + k, t3 + AFTER[f"o{k}+"])
                job = misc(slots, oo, (S("fo"), 2 * b + k + 1))

                def fo(q, b=b, k=k, job=job):
                    m = 2 * b + k
                    q.wait(S("o"), m + 1)
                    q.wait(S("r2"), b + 1)
                    if m >= 2:
                        q.wait(S(f"st_{k}"), 16 * b)
                    q.inc(q.e.tensor_tensor(OUT[:, k, :, :], job["bank"][:, :].rearrange("p (i c) -> p i c", i=2),
                                            Rs[:, b % 4, 2 * k:2 * k + 2, :], ALU.add), S("fo"))
                at("dve", t3 + AFTER[f"fo{k}"], fo)

                def store(q, b=b, k=k):
                    q.wait(S("fo"), 2 * b + k + 1)
                    q.inc(q.e.dma_start(out[b, 256 * k:256 * k + 256, :].rearrange("(i p) c -> p i c", p=128),
                                        OUT[:, k, :, :]), S(f"st_{k}"), 16)
                at("sp", t3 + AFTER[f"st{k}"], store)

        def finish(q):
            for k in range(2):
                q.wait(S(f"st_{k}"), 16 * NB)
            for k in range(2):
                q.wait(S(f"qr_{k}"), 96 * (NB // 2))
                q.wait(S(f"ow_{k}"), 16 * (2 * NB - 1))
        at("sp", 1e9, finish)

        jobs.sort(key=lambda j: j["slots"])
        for n, job in enumerate(jobs):
            job["bank"] = pM[n % 2]
            for part, slot in enumerate(job["slots"]):
                def run(q, n=n, job=job, part=part):
                    if n >= 2 and part == 0:
                        q.wait(*jobs[n - 2]["release"])
                    job["fn"](q, job["bank"], part)
                at("pe", slot + 0.15, run)

        block = ctx.enter_context(nc.Block())

        @block.tensor
        def _(e):
            plan.emit("pe", e)

        @block.scalar
        def _(e):
            plan.emit("act", e)

        @block.vector
        def _(e):
            plan.emit("dve", e)

        @block.gpsimd
        def _(e):
            plan.emit("pool", e)

        @block.sync
        def _(e):
            plan.emit("sp", e)


def kernel(**inputs):
    import numpy as np
    import concourse.bacc as bacc
    from concourse.bass_utils import run_bass_kernel_spmd

    a = {k: np.asarray(v) for k, v in inputs.items()}
    AA, BB = a["L0_ffn_A"], a["L0_ffn_B"]
    arrays = {
        "x": a["L0_attn_x"],
        "wcat": np.concatenate([a["L0_ffn_wd_w"].T, a["L0_attn_Wkv"].T, a["L0_ffn_w_gate"],
                                BB.reshape(ER, C).T], axis=1),
        "wqT": a["L0_attn_Wq"].T,
        "woT": a["L0_attn_Wo"].T,
        "wtT": a["L0_ffn_wt_w"].T,
        "wtb": a["L0_ffn_wt_b"],
        "bq": a["L0_attn_bq"],
        "bkv": a["L0_attn_bkv"],
        "bo": a["L0_attn_bo"],
        "wdb": a["L0_ffn_wd_b"],
        "As": AA.transpose(0, 2, 1).reshape(ER, NL),
        "Am": AA.transpose(1, 0, 2).reshape(NL, ER),
        "scale": a["L0_ffn_scale"],
    }
    nc = bacc.Bacc("TRN2", target_bir_lowering=False, num_devices=1)
    args, feed = [], {}
    for name, v in arrays.items():
        v = np.ascontiguousarray(v)
        feed[f"in_{name}"] = v
        args.append(nc.dram_tensor(f"in_{name}", v.shape, mybir.dt.from_np(v.dtype), kind="ExternalInput").ap())
    o = nc.dram_tensor("out_0", (NB, T, C), F32, kind="ExternalOutput").ap()
    build(nc, *args, o)
    r = run_bass_kernel_spmd(nc, [feed], core_ids=[0])
    return r.results[0]["out_0"]
```
